# Optimizing a Trainium2 kernel written in Bass

```python
import numpy as np
import jax
import jax.numpy as jnp

def _softmax(x, axis=-1):
    return jax.nn.softmax(x, axis=axis)

def _gelu(x):
    return jax.nn.gelu(x, approximate=True)

def _silu(x):
    return jax.nn.silu(x)

def _sigmoid(x):
    return jax.nn.sigmoid(x)

def _layernorm(x, axis=-1, eps=1e-05):
    m = jnp.mean(x, axis=axis, keepdims=True)
    v = jnp.var(x, axis=axis, keepdims=True)
    return (x - m) / jnp.sqrt(v + eps)

def _scatter_add(tgt, idx, src, axis=0):
    return tgt.at[idx].add(src)

def _segment_sum(src, seg, n):
    return jax.ops.segment_sum(src, seg, n)
kernel_name = 'mk_metaformer_d1_conv_nhwc384_r4_dcdbd2'

def setup_inputs(seed: int=0):
    np.random.seed(seed)
    _w = jnp.asarray

    def _rec_inputs():
        import jax
        import jax.numpy as jnp
        _gk = jax.random.key(seed)
        x = -0.000357 + 1 * jax.random.normal(jax.random.fold_in(_gk, 1), (16, 56, 56, 96), jnp.float32)
        return x
    x = _rec_inputs()

    def _L0_conv_setup():
        import jax, jax.numpy as jnp
        import numpy as np
        WS = 7
        EPS = 1e-05

        def _ln(x, w, b):
            mu = jnp.mean(x, axis=-1, keepdims=True)
            var = jnp.mean((x - mu) ** 2, axis=-1, keepdims=True)
            return (x - mu) / jnp.sqrt(var + EPS) * w + b

        def _mamba(xw, A, Bm, Cm):
            xB = xw @ Bm
            xs = jnp.swapaxes(xB, 0, 1)

            def step(h, xb):
                h = xb + h @ A
                return (h, h)
            h0 = jnp.zeros_like(xs[0])
            _, hs = jax.lax.scan(step, h0, xs)
            h = jnp.swapaxes(hs, 0, 1)
            return h @ Cm
        key = jax.random.key(seed)
        ks = jax.random.split(key, 12)
        dim = 96
        hid = 4 * dim
        s = 1.0 / np.sqrt(dim)
        d = {}
        d['x'] = jax.random.normal(ks[0], (16, 56, 56, dim), jnp.float32)
        d['A'] = jax.random.normal(ks[1], (dim, dim), jnp.float32) * (1.0 / dim)
        d['Bm'] = jax.random.normal(ks[2], (dim, dim), jnp.float32) * s
        d['Cm'] = jax.random.normal(ks[3], (dim, dim), jnp.float32) * s
        d['ln1_w'] = jnp.ones((dim,), jnp.float32)
        d['ln1_b'] = jnp.zeros((dim,), jnp.float32)
        d['ln2_w'] = jnp.ones((dim,), jnp.float32)
        d['ln2_b'] = jnp.zeros((dim,), jnp.float32)
        d['W1'] = jax.random.normal(ks[4], (dim, hid), jnp.float32) * s
        d['b1'] = jnp.zeros((hid,), jnp.float32)
        d['W2'] = jax.random.normal(ks[5], (hid, dim), jnp.float32) * (1.0 / np.sqrt(hid))
        d['b2'] = jnp.zeros((dim,), jnp.float32)
        return d
    _L0_conv_all = _L0_conv_setup()
    _L0_conv_in = {k: v for k, v in _L0_conv_all.items() if k in ('A', 'Bm', 'Cm', 'ln1_w', 'ln1_b', 'ln2_w', 'ln2_b', 'W1', 'b1', 'W2', 'b2')}
    del _L0_conv_all

    def _L0_ffn_setup():
        import jax, jax.numpy as jnp
        import numpy as np
        NUM_EXPERTS = 4
        TOP_K = 2
        DIM = 96
        HID = 4 * DIM
        key = jax.random.key(seed)
        ks = jax.random.split(key, 5)
        B, S = (16, 512)
        scale_in = 1.0 / np.sqrt(DIM)
        scale_hid = 1.0 / np.sqrt(HID)
        return {'x': jax.random.normal(ks[0], (B, S, DIM), dtype=jnp.float32), 'gate_w': jax.random.normal(ks[1], (DIM, NUM_EXPERTS), dtype=jnp.float32) * scale_in, 'gate_b': jnp.zeros((NUM_EXPERTS,), dtype=jnp.float32), 'w1': jax.random.normal(ks[2], (NUM_EXPERTS, DIM, HID), dtype=jnp.float32) * scale_in, 'b1': jnp.zeros((NUM_EXPERTS, HID), dtype=jnp.float32), 'w2': jax.random.normal(ks[3], (NUM_EXPERTS, HID, DIM), dtype=jnp.float32) * scale_hid, 'b2': jnp.zeros((NUM_EXPERTS, DIM), dtype=jnp.float32)}
    _L0_ffn_all = _L0_ffn_setup()
    _L0_ffn_in = {k: v for k, v in _L0_ffn_all.items() if k in ('gate_w', 'gate_b', 'w1', 'b1', 'w2', 'b2')}
    del _L0_ffn_all
    return {'x': x, 'L0_conv_A': _L0_conv_in['A'], 'L0_conv_Bm': _L0_conv_in['Bm'], 'L0_conv_Cm': _L0_conv_in['Cm'], 'L0_conv_ln1_w': _L0_conv_in['ln1_w'], 'L0_conv_ln1_b': _L0_conv_in['ln1_b'], 'L0_conv_ln2_w': _L0_conv_in['ln2_w'], 'L0_conv_ln2_b': _L0_conv_in['ln2_b'], 'L0_conv_W1': _L0_conv_in['W1'], 'L0_conv_b1': _L0_conv_in['b1'], 'L0_conv_W2': _L0_conv_in['W2'], 'L0_conv_b2': _L0_conv_in['b2'], 'L0_ffn_gate_w': _L0_ffn_in['gate_w'], 'L0_ffn_gate_b': _L0_ffn_in['gate_b'], 'L0_ffn_w1': _L0_ffn_in['w1'], 'L0_ffn_b1': _L0_ffn_in['b1'], 'L0_ffn_w2': _L0_ffn_in['w2'], 'L0_ffn_b2': _L0_ffn_in['b2']}

def reference(x, L0_conv_A, L0_conv_Bm, L0_conv_Cm, L0_conv_ln1_w, L0_conv_ln1_b, L0_conv_ln2_w, L0_conv_ln2_b, L0_conv_W1, L0_conv_b1, L0_conv_W2, L0_conv_b2, L0_ffn_gate_w, L0_ffn_gate_b, L0_ffn_w1, L0_ffn_b1, L0_ffn_w2, L0_ffn_b2):
    import jax
    import jax.numpy as jnp

    def _L0_conv_ref(x, A, Bm, Cm, ln1_w, ln1_b, ln2_w, ln2_b, W1, b1, W2, b2):
        import jax, jax.numpy as jnp
        import numpy as np
        WS = 7
        EPS = 1e-05

        def _ln(x, w, b):
            mu = jnp.mean(x, axis=-1, keepdims=True)
            var = jnp.mean((x - mu) ** 2, axis=-1, keepdims=True)
            return (x - mu) / jnp.sqrt(var + EPS) * w + b

        def _mamba(xw, A, Bm, Cm):
            xB = xw @ Bm
            xs = jnp.swapaxes(xB, 0, 1)

            def step(h, xb):
                h = xb + h @ A
                return (h, h)
            h0 = jnp.zeros_like(xs[0])
            _, hs = jax.lax.scan(step, h0, xs)
            h = jnp.swapaxes(hs, 0, 1)
            return h @ Cm
        Bn, H, W, C = x.shape
        ws = WS
        w = x.reshape(Bn, H // ws, ws, W // ws, ws, C)
        w = w.transpose(0, 1, 3, 2, 4, 5).reshape(-1, ws * ws, C)
        w = _ln(w, ln1_w, ln1_b)
        w = _mamba(w, A, Bm, Cm)
        xr = w.reshape(Bn, H // ws, W // ws, ws, ws, C)
        xr = xr.transpose(0, 1, 3, 2, 4, 5).reshape(Bn, H, W, C)
        y = _ln(xr, ln2_w, ln2_b)
        y = jax.nn.gelu(y @ W1 + b1, approximate=False) @ W2 + b2
        return xr + y

    def _L0_ffn_ref(x, gate_w, gate_b, w1, b1, w2, b2):
        import jax, jax.numpy as jnp
        import numpy as np
        NUM_EXPERTS = 4
        TOP_K = 2
        DIM = 96
        HID = 4 * DIM
        scores = jnp.einsum('bsd,de->bse', x, gate_w) + gate_b
        probs = jax.nn.softmax(scores, axis=-1)
        topk_vals, topk_idx = jax.lax.top_k(probs, TOP_K)
        mask = jnp.sum(jax.nn.one_hot(topk_idx, NUM_EXPERTS, dtype=probs.dtype), axis=-2)
        masked = probs * mask
        masked = masked / (jnp.sum(masked, axis=-1, keepdims=True) + 1e-09)
        h = jax.nn.gelu(jnp.einsum('bsd,edh->ebsh', x, w1) + b1[:, None, None, :], approximate=False)
        y = jnp.einsum('ebsh,ehd->ebsd', h, w2) + b2[:, None, None, :]
        out = jnp.einsum('bse,ebsd->bsd', masked, y)
        return out

    def _gn(v, G=32, eps=1e-05):
        B_, H_, W_, C_ = v.shape
        g = v.reshape(B_, H_, W_, G, C_ // G)
        m = jnp.mean(g, axis=(1, 2, 4), keepdims=True)
        s = jnp.var(g, axis=(1, 2, 4), keepdims=True)
        return ((g - m) / jnp.sqrt(s + eps)).reshape(v.shape)

    def _ln_c(v, eps=1e-06):
        m = jnp.mean(v, axis=-1, keepdims=True)
        s = jnp.var(v, axis=-1, keepdims=True)
        return (v - m) / jnp.sqrt(s + eps)

    def _ln_t(v, eps=1e-05):
        m = jnp.mean(v, axis=-1, keepdims=True)
        s = jnp.var(v, axis=-1, keepdims=True)
        return (v - m) / jnp.sqrt(s + eps)

    def _to_tokens(v):
        B_, H_, W_, C_ = v.shape
        return v.reshape(B_, H_ * W_, C_)

    def _from_tokens(t, like):
        return t.reshape(like.shape)
    x = x + _L0_conv_ref(_ln_c(x), L0_conv_A, L0_conv_Bm, L0_conv_Cm, L0_conv_ln1_w, L0_conv_ln1_b, L0_conv_ln2_w, L0_conv_ln2_b, L0_conv_W1, L0_conv_b1, L0_conv_W2, L0_conv_b2)
    t = _to_tokens(x)
    t = t + _L0_ffn_ref(_ln_t(t), L0_ffn_gate_w, L0_ffn_gate_b, L0_ffn_w1, L0_ffn_b1, L0_ffn_w2, L0_ffn_b2)
    x = _from_tokens(t, x)
    return x

_drawn_inputs = setup_inputs


def setup_inputs(seed=0):
    import zlib

    import numpy as np

    out = dict(_drawn_inputs(seed))
    spreads = {'L0_conv_ln1_w': (1.0, 0.2),
     'L0_conv_ln1_b': (0.0, 0.1),
     'L0_conv_ln2_w': (1.0, 0.2),
     'L0_conv_ln2_b': (0.0, 0.1),
     'L0_conv_b1': (0.0, 0.1),
     'L0_conv_b2': (0.0, 0.1),
     'L0_ffn_gate_b': (0.0, 0.1),
     'L0_ffn_b1': (0.0, 0.1),
     'L0_ffn_b2': (0.0, 0.1)}
    factors = {}
    for name, (base, spread) in spreads.items():
        noise = np.random.default_rng([zlib.crc32(name.encode()), seed]).standard_normal(out[name].shape)
        drawn = base * np.exp(spread * noise) if base else spread * noise
        out[name] = jnp.asarray(drawn.astype(out[name].dtype))
    for name, factor in factors.items():
        out[name] = (out[name] * factor).astype(out[name].dtype)
    return out
```

```python
from contextlib import ExitStack

import concourse.bass as bass
from concourse import mybir

F32 = mybir.dt.float32
F32R = mybir.dt.float32r
ALU = mybir.AluOpType
ACT = mybir.ActivationFunctionType
AX_X = mybir.AxisListType.X

P = 128
WIN = 7
TILES = WIN * WIN
SUBS = 8
C = 96
TOK = SUBS * P
BANK = 512
HID = 384
KB = HID // P
EXPERTS = 4
SLOTS = KB * (1 + EXPERTS)
KR = C + 2

EPS_C, EPS_1, EPS_T = 1e-6, 1e-5, 1e-5

COL_B, COL_W1, COL_E = 0, C, C + HID
COL_G = COL_E + EXPERTS * HID
WCOLS = COL_G + 2 * EXPERTS

HI_ON_ACT = (0, 2, 4, 6, 8, 10, 12, 14)
HI_ON_DVE = tuple(s for s in range(SLOTS) if s not in HI_ON_ACT)

GATE_STEPS = 14
LN_STEPS = 4
MOMENT_STEPS = 3


class Period:

    def __init__(self, p, par=None):
        self.number = isinstance(p, int)
        self.p = p
        self.par = p % 2 if par is None else par
        has = lambda t: not self.number or 0 <= t < TILES
        self.final = has(p - 1)
        self.experts = has(p)
        self.mlp = has(p + 1)
        self.recur = has(p + 2)
        self.first_ln = has(p + 3)

    def next(self):
        return Period(self.p + 1, 1 - self.par) if not self.number else Period(self.p + 1)

    def has_unit(self, s):
        return self.mlp if s < KB else self.experts

    def unit(self, s):
        if self.number and self.p < 0:
            return s
        if self.number and self.p == TILES - 1:
            return KB + SLOTS * self.p - KB + s
        return SLOTS * self.p + KB + s

    def up_buf(self, s):
        if self.number and self.p == TILES - 1:
            return self.unit(s) % 2
        return (KB + SLOTS * self.par + s) % 2

    def before(self, s, slots):
        mlp, here = sum(x < KB for x in slots), sum(x < s for x in slots)
        if self.number and self.p < 0:
            return here
        if self.number and self.p == TILES - 1:
            return len(slots) * self.p + here
        return len(slots) * self.p + mlp + here

    def group(self, g):
        if self.number and self.p < 0:
            return 0
        if self.number and self.p == TILES - 1:
            return 5 * self.p + g
        return 5 * self.p + 1 + g

    def last_group(self):
        if self.number and self.p == TILES:
            return 5 * (self.p - 1) + EXPERTS
        return 5 * self.p


def periods(eng):
    for p in range(-3, 1):
        yield Period(p)
    with eng.Fori(1, TILES - 5, 2) as p:
        yield Period(p, 1)
        yield Period(p + 1, 0)
    for p in range(TILES - 4, TILES + 1):
        yield Period(p)


def build_program(nc, x, A, Bm, Cm, ln1_w, ln1_b, ln2_w, ln2_b, W1, b1, W2, b2,
                  gate_w, gate_b, ew1, eb1, ew2, eb2, out):
    ctx = ExitStack()

    def sb(name, shape, dt=F32):
        return ctx.enter_context(nc.sbuf_tensor(name, shape, dt))

    def sem(name):
        return ctx.enter_context(nc.semaphore(name))

    with ctx:
        up_ps = ctx.enter_context(nc.psum_tensor("up_ps", [P, 2, TOK], F32))
        y_ps = ctx.enter_context(nc.psum_tensor("y_ps", [P, TOK], F32))
        misc = ctx.enter_context(nc.psum_tensor("misc", [P, TOK], F32))
        misc_tok = misc[:, :].rearrange("p (b n) -> p b n", b=2)[:, :, 0:4 * C]

        w_raw = sb("w_raw", [C, COL_G + EXPERTS])
        w_sc = sb("w_sc", [C, COL_E])
        w_hi = sb("w_hi", [KR, WCOLS], F32R)
        w_lo = sb("w_lo", [C, WCOLS], F32R)
        b_row = sb("b_row", [1, WCOLS])
        b_hi = sb("b_hi", [1, WCOLS], F32R)
        b_lo = sb("b_lo", [1, WCOLS], F32R)
        b1_row = sb("b1_row", [1, HID])
        a_raw = sb("a_raw", [C, 2, C])
        a_hi = sb("a_hi", [C, 2, C], F32R)
        a_lo = sb("a_lo", [C, 2, C], F32R)
        d_raw = sb("d_raw", [P, SLOTS, C])
        d_hi = sb("d_hi", [P, SLOTS, C], F32R)
        d_lo = sb("d_lo", [P, SLOTS, C], F32R)
        b2_col = sb("b2_col", [C, 1 + EXPERTS])
        ln_col = sb("ln_col", [C, 4])
        ident = sb("ident", [P, P])
        neg_half = sb("neg_half", [P, SUBS])
        euler = sb("euler", [P, SUBS * EXPERTS])
        before = sb("before", [P, EXPERTS, EXPERTS])
        x_in = sb("x_in", [P, 2, SUBS, C])
        x_n = sb("x_n", [P, SUBS, C])
        xr = sb("xr", [P, SUBS, C])
        xr_n = sb("xr_n", [P, SUBS, C])
        x_xr = sb("x_xr", [P, SUBS, C])
        acc = sb("acc", [P, 2, SUBS, C])
        acc_n = sb("acc_n", [P, SUBS, C])
        weighted = sb("weighted", [P, SUBS, C])
        out_sb = sb("out_sb", [P, 2, SUBS, C])
        stats = sb("stats", [P, 3, SUBS, 6])
        apart = sb("apart", [P, 3, SUBS])
        mean2 = sb("mean2", [P, 3, SUBS])
        sq_dev = sb("sq_dev", [P, 3, SUBS])
        neg_mean = sb("neg_mean", [P, 3, SUBS])
        var_eps = sb("var_eps", [P, 3, SUBS])
        rstd = sb("rstd", [P, 3, SUBS])
        x_hi = sb("x_hi", [KR, TOK], F32R)
        x_lo = sb("x_lo", [C, TOK], F32R)
        h_hi = sb("h_hi", [C, TOK], F32R)
        h_lo = sb("h_lo", [C, TOK], F32R)
        y_hi = sb("y_hi", [KR, TOK], F32R)
        y_lo = sb("y_lo", [C, TOK], F32R)
        t_hi = sb("t_hi", [KR, 2, TOK], F32R)
        t_lo = sb("t_lo", [C, 2, TOK], F32R)
        g = sb("g", [P, 3, TOK])
        g_hi = sb("g_hi", [P, 3, TOK], F32R)
        g_lo = sb("g_lo", [P, 3, TOK], F32R)
        y_sb = sb("y_sb", [C, TOK])
        score = sb("score", [P, SUBS, EXPERTS])
        top = sb("top", [P, SUBS])
        below = sb("below", [P, SUBS, EXPERTS])
        ex = sb("ex", [P, SUBS, EXPERTS])
        more = sb("more", [P, SUBS, EXPERTS, EXPERTS])
        same = sb("same", [P, SUBS, EXPERTS, EXPERTS])
        rank = sb("rank", [P, SUBS, EXPERTS])
        kept = sb("kept", [P, SUBS, EXPERTS])
        sum_all = sb("sum_all", [P, SUBS])
        sum_kept = sb("sum_kept", [P, SUBS])
        denom = sb("denom", [P, SUBS])
        inv = sb("inv", [P, SUBS])
        weight = sb("weight", [P, 2, SUBS, EXPERTS])

        w_loaded = sem("w_loaded")
        bias_rows = sem("bias_rows")
        x_loaded = [sem("x_loaded0"), sem("x_loaded1")]
        stored = [sem("stored0"), sem("stored1")]
        const_step = sem("const_step")
        prep = sem("prep")
        rows_set = sem("rows_set")
        bias_sums = sem("bias_sums")
        up_done, down_done = sem("up_done"), sem("down_done")
        x_turned, xr_turned, acc_turned = sem("x_turned"), sem("xr_turned"), sem("acc_turned")
        h_summed, xr_summed, scored = sem("h_summed"), sem("xr_summed"), sem("scored")
        y_turned = sem("y_turned")
        gelu_done, act_hi_done, y_copied = sem("gelu_done"), sem("act_hi_done"), sem("y_copied")
        x_hi_ok, h_hi_ok, y_hi_ok, t_hi_ok = sem("x_hi_ok"), sem("h_hi_ok"), sem("y_hi_ok"), sem("t_hi_ok")
        xr_copied = sem("xr_copied")
        dve_hi_done, lo_done = sem("dve_hi_done"), sem("lo_done")
        x_lo_ok, h_lo_ok, y_lo_ok, t_lo_ok = sem("x_lo_ok"), sem("h_lo_ok"), sem("y_lo_ok"), sem("t_lo_ok")
        stats_ok = [sem(f"stats_ok{k}") for k in range(3)]
        moments_ok = [sem(f"moments_ok{k}") for k in range(3)]
        x_xr_ok, x2_ok = sem("x_xr_ok"), sem("x2_ok")
        weighted_ok, summed = sem("weighted_ok"), sem("summed")
        gate_step = sem("gate_step")
        ln_step = [sem(f"ln_step{k}") for k in range(3)]
        normed = [sem(f"normed{k}") for k in range(3)]
        ex_ok = sem("ex_ok")

        W_PARTS = 18
        CONSTS = 8

        block = ctx.enter_context(nc.Block())

        @block.sync
        def _(sp):
            def load(t, par):
                sp.dma_start(x_in[:, par, :, :].rearrange("p s c -> p (s c)"), x[t, :, :]).then_inc(x_loaded[par], 16)

            def store(t, par):
                sp.wait_ge(summed, EXPERTS * t + EXPERTS)
                sp.dma_start(out[t, :, :], out_sb[:, par, :, :].rearrange("p s c -> p (s c)")).then_inc(stored[par], 16)

            def reload(t, par):
                sp.wait_ge(x_xr_ok, t - 1)
                load(t, par)

            load(0, 0)
            load(1, 1)
            for t in (2, 3, 4):
                reload(t, t % 2)
            with sp.Fori(1, TILES - 5, 2) as p:
                store(p - 1, 0)
                reload(p + 4, 1)
                store(p, 1)
                reload(p + 5, 0)
            for t in range(TILES - 5, TILES):
                store(t, t % 2)
            sp.wait_ge(stored[0], 16 * ((TILES + 1) // 2))
            sp.wait_ge(stored[1], 16 * (TILES // 2))

        @block.gpsimd
        def _(pool):
            pool.memset(ident[:, :], 0.0).then_inc(const_step, 1)
            pool.wait_ge(const_step, 1)
            pool.affine_select(out=ident[:, :], in_=ident[:, :], compare_op=ALU.not_equal, fill=1.0,
                               base=0, pattern=[[-1, P]], channel_multiplier=1).then_inc(const_step, 1)
            pool.memset(neg_half[:, :], -0.5).then_inc(const_step, 1)
            pool.memset(euler[:, :], 2.718281828459045).then_inc(const_step, 1)
            pool.memset(before[:, :, :], 0.0).then_inc(const_step, 1)
            pool.wait_ge(const_step, 5)
            for i in range(1, EXPERTS):
                pool.memset(before[:, i, 0:i], 1.0).then_inc(const_step, 1)
            pool.wait_ge(const_step, CONSTS)

            def per_token(ap):
                return ap.unsqueeze(2).to_broadcast([P, SUBS, C])

            def normalise(k, t, src, dst, turned, scale, eps):
                pool.wait_ge(moments_ok[k], t + 1)
                pool.tensor_tensor(neg_mean[:, k, :], mean2[:, k, :], neg_half[:, :], ALU.mult).then_inc(ln_step[k], 1)
                pool.tensor_scalar(var_eps[:, k, :], sq_dev[:, k, :], scale / C, eps, ALU.mult, ALU.add).then_inc(ln_step[k], 1)
                pool.wait_ge(ln_step[k], LN_STEPS * t + 2)
                pool.tensor_tensor(rstd[:, k, :], var_eps[:, k, :], neg_half[:, :], ALU.pow).then_inc(ln_step[k], 1)
                if not (isinstance(t, int) and t == 0):
                    pool.wait_ge(turned, t)
                pool.tensor_tensor(dst[:, :, :], src, per_token(neg_mean[:, k, :]), ALU.add).then_inc(ln_step[k], 1)
                pool.wait_ge(ln_step[k], LN_STEPS * t + 4)
                pool.tensor_tensor(dst[:, :, :], dst[:, :, :], per_token(rstd[:, k, :]), ALU.mult).then_inc(normed[k], 1)

            for q in periods(pool):
                if q.mlp:
                    normalise(2, q.p + 1, acc[:, 1 - q.par, :, :], acc_n, acc_turned, 1.0, EPS_T)
                if q.first_ln:
                    normalise(0, q.p + 3, x_in[:, 1 - q.par, :, :], x_n, x_turned, 1.0 + EPS_1, EPS_C * EPS_1)
                if q.recur:
                    normalise(1, q.p + 2, xr[:, :, :], xr_n, xr_turned, 1.0, EPS_1)
                if q.mlp:
                    t = q.p + 1
                    pool.wait_ge(gate_step, GATE_STEPS * t + 3)
                    pool.tensor_tensor(ex[:, :, :].rearrange("p s e -> p (s e)"), euler[:, :],
                                       below[:, :, :].rearrange("p s e -> p (s e)"), ALU.pow).then_inc(ex_ok, 1)

        @block.scalar
        def _(act):
            act.dma_start(w_raw[:, COL_B:COL_W1], Bm[:, :]).then_inc(w_loaded, 16)
            act.dma_start(w_raw[:, COL_W1:COL_E], W1[:, :]).then_inc(w_loaded, 16)
            act.dma_start(w_raw[:, COL_E:COL_G].rearrange("d (e h) -> d e h", e=EXPERTS),
                          ew1.rearrange("e d h -> d e h")).then_inc(w_loaded, 16)
            act.dma_start(w_raw[:, COL_G:COL_G + EXPERTS], gate_w[:, :]).then_inc(w_loaded, 16)
            act.dma_start(a_raw[:, 0, :], A[:, :]).then_inc(w_loaded, 16)
            act.dma_start(a_raw[:, 1, :], Cm[:, :]).then_inc(w_loaded, 16)
            act.dma_start(d_raw[:, 0:KB, :], W2.rearrange("(k p) c -> p k c", p=P)).then_inc(w_loaded, 16)
            for e in range(EXPERTS):
                act.dma_start(d_raw[:, KB * (1 + e):KB * (2 + e), :],
                              ew2[e, :, :].rearrange("(k p) c -> p k c", p=P)).then_inc(w_loaded, 16)
            act.dma_start(b2_col[:, 0:1], b2[:, :]).then_inc(w_loaded, 16)
            act.dma_start(b2_col[:, 1:1 + EXPERTS], eb2[:, :]).then_inc(w_loaded, 16)
            for i, v in enumerate((ln1_w, ln1_b, ln2_w, ln2_b)):
                act.dma_start(ln_col[:, i:i + 1], v[:, :]).then_inc(w_loaded, 16)
            act.dma_start(b1_row[:, :], b1[:, :]).then_inc(w_loaded, 16)
            act.dma_start(b_row[:, COL_E:COL_G], eb1[:, :]).then_inc(w_loaded, 16)
            act.dma_start(b_row[:, COL_G:COL_G + EXPERTS], gate_b[:, :]).then_inc(w_loaded, 16)
            act.wait_ge(prep, W_PARTS)
            act.dma_start(w_hi[C:C + 1, :].bitcast(F32), b_hi[:, :].bitcast(F32)).then_inc(bias_rows, 16)
            act.dma_start(w_hi[C + 1:KR, :].bitcast(F32), b_lo[:, :].bitcast(F32)).then_inc(bias_rows, 16)

            def gelu(q, s):
                n, r, u = q.unit(s), s % 3, q.up_buf(s)
                act.wait_ge(up_done, n + 1)
                if not (q.number and n < 3):
                    act.wait_ge(lo_done, n - 2)
                act.activation(g[:, r, :], up_ps[:, u, :], ACT.Gelu).then_inc(gelu_done, 1)
                if s in HI_ON_ACT:
                    act.wait_ge(gelu_done, n + 1)
                    if not (q.number and n < 3):
                        act.wait_ge(down_done, n - 2)
                    act.copy(g_hi[:, r, :], g[:, r, :]).then_inc(act_hi_done, 1)

            def hi_part(t, made, dst, done):
                act.wait_ge(made, t + 1)
                act.copy(dst, misc[0:C, :]).then_inc(done, 1)

            for q in periods(act):
                for s in range(SLOTS):
                    nx = q.next()
                    if s + 2 < SLOTS:
                        if q.has_unit(s + 2):
                            gelu(q, s + 2)
                    elif q.recur:
                        gelu(nx, s + 2 - SLOTS)
                    if s % KB == KB - 1 and q.has_unit(s):
                        grp = s // KB
                        n = q.group(grp)
                        act.wait_ge(down_done, q.unit(s) + 1)
                        if not (q.number and n == 0):
                            act.wait_ge(y_turned, n)
                        act.activation(y_sb[:, :], y_ps[0:C, :], ACT.Identity,
                                       bias=b2_col[:, grp:grp + 1]).then_inc(y_copied, 1)
                    if s == 1 and q.recur:
                        hi_part(q.p + 2, x_turned, x_hi[0:C, :], x_hi_ok)
                    if s == 4 and q.recur:
                        hi_part(q.p + 2, h_summed, h_hi[:, :], h_hi_ok)
                    if s == 7 and q.recur:
                        act.wait_ge(xr_summed, q.p + 3)
                        act.copy(xr[:, :, :].rearrange("p (b s) c -> p b (s c)", b=2), misc_tok).then_inc(xr_copied, 1)
                    if s == 8 and q.mlp:
                        hi_part(q.p + 1, acc_turned, t_hi[0:C, 1 - q.par, :], t_hi_ok)
                    if s == 11 and q.recur:
                        hi_part(q.p + 2, xr_turned, y_hi[0:C, :], y_hi_ok)

        @block.vector
        def _(dve):
            def f(ap):
                return ap.bitcast(F32)

            for rows in (x_hi[C:KR, :], y_hi[C:KR, :], t_hi[C:KR, 0, :], t_hi[C:KR, 1, :]):
                dve.memset(f(rows), 1.0).then_inc(rows_set, 1)
            for state in (h_hi, h_lo):
                dve.memset(f(state[:, :]), 0.0).then_inc(rows_set, 1)

            done = [0]

            def part(ins):
                done[0] += 1
                ins.then_inc(prep, 1)

            dve.wait_ge(w_loaded, 16 * 20)
            part(dve.tensor_scalar(w_sc[:, COL_B:COL_W1], w_raw[:, COL_B:COL_W1], ln_col[:, 0:1], None, ALU.mult))
            part(dve.tensor_scalar(w_sc[:, COL_W1:COL_E], w_raw[:, COL_W1:COL_E], ln_col[:, 2:3], None, ALU.mult))
            part(dve.memset(b_row[:, COL_G + EXPERTS:WCOLS], 0.0))
            part(dve.memset(f(w_lo[:, COL_G + EXPERTS:WCOLS]), 0.0))
            part(dve.tensor_copy(w_hi[0:C, COL_E:COL_G + EXPERTS], w_raw[:, COL_E:COL_G + EXPERTS]))
            part(dve.tensor_copy(w_lo[:, COL_G:COL_G + EXPERTS], w_raw[:, COL_G:COL_G + EXPERTS]))
            part(dve.tensor_copy(a_hi[:, :, :], a_raw[:, :, :]))
            part(dve.tensor_copy(d_hi[:, :, :], d_raw[:, :, :]))
            dve.wait_ge(prep, 2)
            part(dve.tensor_copy(w_hi[0:C, 0:COL_E], w_sc[:, :]))
            dve.wait_ge(prep, 9)
            part(dve.tensor_tensor(w_lo[:, 0:COL_E], w_sc[:, :], f(w_hi[0:C, 0:COL_E]), ALU.subtract))
            part(dve.tensor_tensor(w_lo[:, COL_E:COL_G], w_raw[:, COL_E:COL_G], f(w_hi[0:C, COL_E:COL_G]), ALU.subtract))
            part(dve.tensor_tensor(w_hi[0:C, COL_G + EXPERTS:WCOLS], w_raw[:, COL_G:COL_G + EXPERTS],
                                   f(w_hi[0:C, COL_G:COL_G + EXPERTS]), ALU.subtract))
            part(dve.tensor_tensor(a_lo[:, :, :], a_raw[:, :, :], f(a_hi[:, :, :]), ALU.subtract))
            part(dve.tensor_tensor(d_lo[:, :, :], d_raw[:, :, :], f(d_hi[:, :, :]), ALU.subtract))
            dve.wait_ge(bias_sums, 1)
            part(dve.tensor_copy(b_row[:, COL_B:COL_W1], misc[0:1, 0:C]))
            part(dve.tensor_tensor(b_row[:, COL_W1:COL_E], misc[0:1, BANK:BANK + HID], b1_row[:, :], ALU.add))
            dve.wait_ge(prep, 16)
            part(dve.tensor_copy(b_hi[:, :], b_row[:, :]))
            dve.wait_ge(prep, 17)
            part(dve.tensor_tensor(b_lo[:, :], b_row[:, :], f(b_hi[:, :]), ALU.subtract))
            assert done[0] == W_PARTS
            dve.wait_ge(const_step, CONSTS)

            def unit_lo(q, s):
                n, r = q.unit(s), s % 3
                if s in HI_ON_ACT:
                    dve.wait_ge(act_hi_done, q.before(s, HI_ON_ACT) + 1)
                    dve.tensor_tensor(g_lo[:, r, :], g[:, r, :], f(g_hi[:, r, :]), ALU.subtract).then_inc(lo_done, 1)
                else:
                    dve.wait_ge(gelu_done, n + 1)
                    if not (q.number and n < 3):
                        dve.wait_ge(down_done, n - 2)
                    dve.tensor_copy(g_hi[:, r, :], g[:, r, :]).then_inc(dve_hi_done, 1)
                    dve.wait_ge(dve_hi_done, q.before(s, HI_ON_DVE) + 1)
                    dve.tensor_tensor(g_lo[:, r, :], g[:, r, :], f(g_hi[:, r, :]), ALU.subtract).then_inc(lo_done, 1)

            def lo_part(t, hi_ok, hi, lo, lo_ok):
                dve.wait_ge(hi_ok, t + 1)
                dve.tensor_tensor(lo, misc[0:C, :], f(hi), ALU.subtract).then_inc(lo_ok, 1)

            def moments(k, t, src):
                for s in range(SUBS):
                    ins = dve.bn_stats(stats[:, k, s, :], src[:, s, :])
                ins.then_inc(stats_ok[k], 1)
                dve.wait_ge(stats_ok[k], MOMENT_STEPS * t + 1)
                mean_e, dev_e, mean_o, dev_o = (stats[:, k, :, i] for i in (1, 2, 4, 5))
                dve.tensor_tensor(apart[:, k, :], mean_e, mean_o, ALU.subtract).then_inc(stats_ok[k], 1)
                if not (isinstance(t, int) and t == 0):
                    dve.wait_ge(normed[k], t)
                dve.tensor_tensor(mean2[:, k, :], mean_e, mean_o, ALU.add)
                dve.wait_ge(stats_ok[k], MOMENT_STEPS * t + 2)
                dve.scalar_tensor_tensor(apart[:, k, :], in0=apart[:, k, :], scalar=C / 4, in1=apart[:, k, :],
                                         op0=ALU.mult, op1=ALU.mult)
                dve.tensor_tensor(sq_dev[:, k, :], dev_e, dev_o, ALU.add).then_inc(stats_ok[k], 1)
                dve.wait_ge(stats_ok[k], MOMENT_STEPS * t + 3)
                dve.tensor_tensor(sq_dev[:, k, :], sq_dev[:, k, :], apart[:, k, :], ALU.add).then_inc(moments_ok[k], 1)

            def tok4(ap):
                return ap.rearrange("p (b s) c -> p b s c", b=2)

            def combine(t, par, e, turned):
                w = weight[:, par, :, e].rearrange("p (b s) -> p b s", b=2).unsqueeze(3).to_broadcast([P, 2, 4, C])
                if not (isinstance(t, int) and t == 0 and e == 0):
                    dve.wait_ge(summed, EXPERTS * t + e)
                dve.wait_ge(y_turned, turned + 1)
                dve.tensor_tensor(tok4(weighted[:, :, :]), misc_tok.rearrange("p b (s c) -> p b s c", s=4), w,
                                  ALU.mult).then_inc(weighted_ok, 1)
                dve.wait_ge(weighted_ok, EXPERTS * t + e + 1)
                if e < EXPERTS - 1:
                    dst = acc
                else:
                    dst = out_sb
                    if not (isinstance(t, int) and t < 2):
                        dve.wait_ge(stored[par], 8 * (t - par))
                dve.tensor_tensor(dst[:, par, :, :], acc[:, par, :, :], weighted[:, :, :], ALU.add).then_inc(summed, 1)

            def gate(t, par):
                base, k = GATE_STEPS * t, [0]

                def step(ins):
                    k[0] += 1
                    ins.then_inc(gate_step, 1)

                def after(n):
                    dve.wait_ge(gate_step, base + n)

                by_i = score[:, :, :].unsqueeze(3).to_broadcast([P, SUBS, EXPERTS, EXPERTS])
                by_j = score[:, :, :].unsqueeze(2).to_broadcast([P, SUBS, EXPERTS, EXPERTS])
                row = lambda a: a.unsqueeze(2).to_broadcast([P, SUBS, EXPERTS])
                dve.wait_ge(scored, t + 1)
                step(dve.tensor_reduce(score[:, :, :], misc[:, 0:SUBS * 2 * EXPERTS].rearrange(
                    "p (s l e) -> p s e l", s=SUBS, l=2), AX_X, ALU.add))
                after(1)
                step(dve.tensor_reduce(top[:, :], score[:, :, :], AX_X, ALU.max))
                after(2)
                step(dve.tensor_tensor(below[:, :, :], score[:, :, :], row(top[:, :]), ALU.subtract))
                step(dve.tensor_tensor(more[:, :, :, :], by_j, by_i, ALU.is_gt))
                step(dve.tensor_tensor(same[:, :, :, :], by_j, by_i, ALU.is_equal))
                after(5)
                first = before[:, :, :].unsqueeze(1).to_broadcast([P, SUBS, EXPERTS, EXPERTS])
                step(dve.tensor_tensor(same[:, :, :, :], same[:, :, :, :], first, ALU.mult))
                after(6)
                step(dve.tensor_tensor(more[:, :, :, :], more[:, :, :, :], same[:, :, :, :], ALU.add))
                after(7)
                step(dve.tensor_reduce(rank[:, :, :], more[:, :, :, :], AX_X, ALU.add))
                dve.wait_ge(ex_ok, t + 1)
                step(dve.tensor_reduce(sum_all[:, :], ex[:, :, :], AX_X, ALU.add))
                after(8)
                step(dve.scalar_tensor_tensor(kept[:, :, :], in0=rank[:, :, :], scalar=2.0, in1=ex[:, :, :],
                                              op0=ALU.is_lt, op1=ALU.mult))
                after(10)
                step(dve.tensor_reduce(sum_kept[:, :], kept[:, :, :], AX_X, ALU.add))
                after(11)
                step(dve.scalar_tensor_tensor(denom[:, :], in0=sum_all[:, :], scalar=1e-9, in1=sum_kept[:, :],
                                              op0=ALU.mult, op1=ALU.add))
                after(12)
                step(dve.reciprocal(inv[:, :], denom[:, :]))
                after(13)
                step(dve.tensor_tensor(weight[:, par, :, :], kept[:, :, :], row(inv[:, :]), ALU.mult))
                assert k[0] == GATE_STEPS

            for q in periods(dve):
                te, tm, tp, tl = q.p, q.p + 1, q.p + 2, q.p + 3
                par, npar = q.par, 1 - q.par
                for s in range(SLOTS):
                    nx = q.next()
                    if s + 2 < SLOTS:
                        if q.has_unit(s + 2):
                            unit_lo(q, s + 2)
                    elif q.recur:
                        unit_lo(nx, s + 2 - SLOTS)
                    if s == 0 and q.final:
                        combine(te - 1, npar, EXPERTS - 1, q.last_group())
                    if s == 1 and q.recur:
                        lo_part(tp, x_hi_ok, x_hi[0:C, :], x_lo[:, :], x_lo_ok)
                    if s == 3 and q.mlp:
                        dve.wait_ge(y_turned, q.group(0) + 1)
                        dve.tensor_tensor(acc[:, npar, :, :].rearrange("p (b s) c -> p b (s c)", b=2), misc_tok,
                                          x_xr[:, :, :].rearrange("p (b s) c -> p b (s c)", b=2), ALU.add).then_inc(x2_ok, 1)
                        dve.wait_ge(x2_ok, tm + 1)
                        moments(2, tm, acc[:, npar, :, :])
                    if s == 4 and q.recur:
                        lo_part(tp, h_hi_ok, h_hi[:, :], h_lo[:, :], h_lo_ok)
                    if s == 5 and q.first_ln:
                        dve.wait_ge(x_loaded[npar], 8 * (tl - npar) + 16)
                        moments(0, tl, x_in[:, npar, :, :])
                    if s in (6, 9, 12) and q.experts:
                        combine(te, par, s // KB - 2, q.group(s // KB - 1))
                    if s == 7 and q.recur:
                        dve.wait_ge(xr_copied, tp + 1)
                        dve.tensor_tensor(x_xr[:, :, :], xr[:, :, :], x_in[:, par, :, :], ALU.add).then_inc(x_xr_ok, 1)
                        moments(1, tp, xr[:, :, :])
                    if s == 8 and q.mlp:
                        lo_part(tm, t_hi_ok, t_hi[0:C, npar, :], t_lo[:, npar, :], t_lo_ok)
                    if s == 10 and q.mlp:
                        gate(tm, npar)
                    if s == 11 and q.recur:
                        lo_part(tp, y_hi_ok, y_hi[0:C, :], y_lo[:, :], y_lo_ok)

        @block.tensor
        def _(pe):
            pe.wait_ge(w_loaded, 16 * 20)
            pe.matmul(misc[0:1, 0:C], ln_col[:, 1:2], w_raw[:, COL_B:COL_W1], start=True, stop=True)
            pe.matmul(misc[0:1, BANK:BANK + HID], ln_col[:, 3:4], w_raw[:, COL_W1:COL_E],
                      start=True, stop=True).then_inc(bias_sums, 1)
            pe.wait_ge(const_step, CONSTS)
            pe.wait_ge(prep, W_PARTS)
            pe.wait_ge(bias_rows, 32)
            pe.wait_ge(rows_set, 6)

            HALVES = (slice(0, BANK), slice(BANK, TOK))

            def product(dst, rows, terms):
                for i, (w, v) in enumerate(terms):
                    for h in HALVES:
                        ins = pe.matmul(dst[0:rows, h], w, v[:, h], start=(i == 0), stop=(i == len(terms) - 1))
                return ins

            def up(q, s):
                n = q.unit(s)
                if s < KB:
                    hi, lo, col = y_hi[:, :], y_lo[:, :], COL_W1 + P * s
                    if s == 0:
                        pe.wait_ge(y_lo_ok, q.p + 2)
                else:
                    hi, lo, col = t_hi[:, q.par, :], t_lo[:, q.par, :], COL_E + P * (s - KB)
                    if s == KB:
                        pe.wait_ge(t_lo_ok, q.p + 1)
                if not (q.number and n < 2):
                    pe.wait_ge(gelu_done, n - 1)
                c = slice(col, col + P)
                product(up_ps[:, q.up_buf(s), :], P, ((w_hi[:, c], hi), (w_hi[0:C, c], lo),
                                                      (w_lo[:, c], hi[0:C, :]))).then_inc(up_done, 1)

            def down(q, s):
                n, r, grp, k = q.unit(s), s % 3, s // KB, s % KB
                pe.wait_ge(lo_done, n + 1)
                if k == 0 and not (q.number and q.group(grp) == 0):
                    pe.wait_ge(y_copied, q.group(grp))
                terms = ((d_hi[:, s, :], g_hi[:, r, :]), (d_hi[:, s, :], g_lo[:, r, :]), (d_lo[:, s, :], g_hi[:, r, :]))
                for i, (w, v) in enumerate(terms):
                    for h in HALVES:
                        ins = pe.matmul(y_ps[0:C, h], w, v[:, h], start=(k == 0 and i == 0), stop=(k == KB - 1 and i == 2))
                ins.then_inc(down_done, 1)

            freed = [None]

            def use_misc(q, release, value):
                if freed[0] is not None:
                    pe.wait_ge(*freed[0])
                freed[0] = (release, value)

            def to_channels(src):
                for s in range(SUBS):
                    ins = pe.transpose(misc[0:C, s * P:(s + 1) * P], src[:, s, :], ident[:, :])
                return ins

            def turn_y(n):
                pe.wait_ge(y_copied, n + 1)
                for s in range(SUBS):
                    ins = pe.transpose(misc_tok[:, s // 4, (s % 4) * C:(s % 4 + 1) * C],
                                       y_sb[:, s * P:(s + 1) * P], ident[0:C, 0:C])
                ins.then_inc(y_turned, 1)

            for q in periods(pe):
                te, tm, tp = q.p, q.p + 1, q.p + 2
                par, npar = q.par, 1 - q.par
                if not q.number:
                    freed[0] = (weighted_ok, EXPERTS * (te - 1) + 3)
                if q.number and te == TILES - 4:
                    freed[0] = (weighted_ok, EXPERTS * (te - 1) + 3)
                for s in range(SLOTS):
                    nx = q.next()
                    if s + 2 < SLOTS:
                        if q.has_unit(s + 2):
                            up(q, s + 2)
                    elif q.recur:
                        up(nx, s + 2 - SLOTS)
                    if q.has_unit(s):
                        down(q, s)
                    if s == 0 and q.final:
                        use_misc(q, weighted_ok, EXPERTS * te)
                        turn_y(q.last_group())
                    if s == 1 and q.recur:
                        use_misc(q, x_lo_ok, tp + 1)
                        pe.wait_ge(normed[0], tp + 1)
                        to_channels(x_n).then_inc(x_turned, 1)
                    if s == 3 and q.mlp:
                        use_misc(q, x2_ok, tm + 1)
                        turn_y(q.group(0))
                    if s == 4 and q.recur:
                        use_misc(q, h_lo_ok, tp + 1)
                        pe.wait_ge(x_lo_ok, tp + 1)
                        if not (q.number and tp == 0):
                            pe.wait_ge(h_lo_ok, tp)
                        c = slice(COL_B, COL_W1)
                        product(misc, C, ((w_hi[:, c], x_hi[:, :]), (w_hi[0:C, c], x_lo[:, :]), (w_lo[:, c], x_hi[0:C, :]),
                                          (a_hi[:, 0, :], h_hi[:, :]), (a_hi[:, 0, :], h_lo[:, :]),
                                          (a_lo[:, 0, :], h_hi[:, :]))).then_inc(h_summed, 1)
                    if s in (6, 9, 12) and q.experts:
                        e = s // KB - 2
                        use_misc(q, weighted_ok, EXPERTS * te + e + 1)
                        turn_y(q.group(e + 1))
                    if s == 7 and q.recur:
                        use_misc(q, xr_copied, tp + 1)
                        pe.wait_ge(h_lo_ok, tp + 1)
                        for b in range(SUBS):
                            v = slice(b * P, (b + 1) * P)
                            dst = misc_tok[:, b // 4, (b % 4) * C:(b % 4 + 1) * C]
                            pe.matmul(dst, h_hi[:, v], a_hi[:, 1, :], start=True, stop=False)
                            pe.matmul(dst, h_lo[:, v], a_hi[:, 1, :], start=False, stop=False)
                            ins = pe.matmul(dst, h_hi[:, v], a_lo[:, 1, :], start=False, stop=True)
                        ins.then_inc(xr_summed, 1)
                    if s == 8 and q.mlp:
                        use_misc(q, t_lo_ok, tm + 1)
                        pe.wait_ge(normed[2], tm + 1)
                        to_channels(acc_n).then_inc(acc_turned, 1)
                    if s == 10 and q.mlp:
                        use_misc(q, gate_step, GATE_STEPS * tm + 1)
                        pe.wait_ge(t_lo_ok, tm + 1)
                        c = slice(COL_G, WCOLS)
                        for b in range(SUBS):
                            v = slice(b * P, (b + 1) * P)
                            dst = misc[:, 2 * EXPERTS * b:2 * EXPERTS * (b + 1)]
                            pe.matmul(dst, t_hi[:, npar, v], w_hi[:, c], start=True, stop=False)
                            ins = pe.matmul(dst, t_lo[:, npar, v], w_lo[:, c], start=False, stop=True)
                        ins.then_inc(scored, 1)
                    if s == 11 and q.recur:
                        use_misc(q, y_lo_ok, tp + 1)
                        pe.wait_ge(normed[1], tp + 1)
                        to_channels(xr_n).then_inc(xr_turned, 1)


NAMES = ("x", "L0_conv_A", "L0_conv_Bm", "L0_conv_Cm", "L0_conv_ln1_w", "L0_conv_ln1_b", "L0_conv_ln2_w",
         "L0_conv_ln2_b", "L0_conv_W1", "L0_conv_b1", "L0_conv_W2", "L0_conv_b2", "L0_ffn_gate_w",
         "L0_ffn_gate_b", "L0_ffn_w1", "L0_ffn_b1", "L0_ffn_w2", "L0_ffn_b2")


def kernel(**inputs):
    import numpy as np
    import concourse.bacc as bacc
    from concourse.bass_utils import run_bass_kernel_spmd

    B, H, W, ch = inputs["x"].shape
    a = {n: np.asarray(inputs[n]) for n in NAMES}
    win = a["x"].reshape(B, H // WIN, WIN, W // WIN, WIN, ch).transpose(2, 4, 0, 1, 3, 5)
    a["x"] = win.reshape(TILES, P, SUBS * C)
    for n in ("L0_conv_ln1_w", "L0_conv_ln1_b", "L0_conv_ln2_w", "L0_conv_ln2_b", "L0_conv_b2"):
        a[n] = a[n].reshape(C, 1)
    for n in ("L0_conv_b1", "L0_ffn_gate_b", "L0_ffn_b1"):
        a[n] = a[n].reshape(1, -1)
    a["L0_ffn_b2"] = a["L0_ffn_b2"].T

    nc = bacc.Bacc("TRN2", target_bir_lowering=False, num_devices=1)
    arrays, args = {}, []
    for n in NAMES:
        v = np.ascontiguousarray(a[n])
        arrays[f"in_{n}"] = v
        args.append(nc.dram_tensor(f"in_{n}", v.shape, mybir.dt.from_np(v.dtype), kind="ExternalInput").ap())
    out = nc.dram_tensor("out_0", (TILES, P, SUBS * C), F32, kind="ExternalOutput").ap()
    build_program(nc, *args, out)
    r = run_bass_kernel_spmd(nc, [arrays], core_ids=[0])
    got = np.asarray(r.results[0]["out_0"]).reshape(WIN, WIN, B, H // WIN, W // WIN, ch)
    return np.ascontiguousarray(got.transpose(2, 3, 0, 4, 1, 5)).reshape(B, H, W, ch)
```

```python
from contextlib import ExitStack

import concourse.bass as bass
from concourse import mybir

F32 = mybir.dt.float32
F32R = mybir.dt.float32r
ALU = mybir.AluOpType
ACT = mybir.ActivationFunctionType
AX_X = mybir.AxisListType.X

P = 128
WIN = 7
TILES = WIN * WIN
SUBS = 8
C = 96
TOK = SUBS * P
BANK = 512
HID = 384
KB = HID // P
EXPERTS = 4
SLOTS = KB * (1 + EXPERTS)
KR = C + 2

EPS_C, EPS_1, EPS_T = 1e-6, 1e-5, 1e-5

COL_B, COL_W1, COL_E = 0, C, C + HID
COL_G = COL_E + EXPERTS * HID
WCOLS = COL_G + 2 * EXPERTS

HI_ON_DVE = (1, 4, 7, 10, 13)
HI_ON_ACT = tuple(s for s in range(SLOTS) if s not in HI_ON_DVE)

TURN_EXPERT = (8, 9, 12)
HALVES = (slice(0, BANK), slice(BANK, TOK))

GATE_STEPS = 14
LN_STEPS = 4
MOMENT_STEPS = 3


class Period:

    def __init__(self, p, par=None):
        self.number = isinstance(p, int)
        self.p = p
        self.par = p % 2 if par is None else par
        has = lambda t: not self.number or 0 <= t < TILES
        self.final = has(p - 1)
        self.experts = has(p)
        self.mlp = has(p + 1)
        self.recur = has(p + 2)
        self.first_ln = has(p + 3)

    def next(self):
        return Period(self.p + 1, 1 - self.par) if not self.number else Period(self.p + 1)

    def has_unit(self, s):
        return self.mlp if s < KB else self.experts

    def ahead(self, s):
        if s + 2 < SLOTS:
            return (self, s + 2) if self.has_unit(s + 2) else None
        return (self.next(), s + 2 - SLOTS) if self.recur else None

    def unit(self, s):
        if self.number and self.p < 0:
            return s
        if self.number and self.p == TILES - 1:
            return KB + SLOTS * self.p - KB + s
        return SLOTS * self.p + KB + s

    def up_buf(self, s):
        if self.number and self.p == TILES - 1:
            return self.unit(s) % 2
        return (KB + SLOTS * self.par + s) % 2

    def before(self, s, slots):
        mlp, here = sum(x < KB for x in slots), sum(x < s for x in slots)
        if self.number and self.p < 0:
            return here
        if self.number and self.p == TILES - 1:
            return len(slots) * self.p + here
        return len(slots) * self.p + mlp + here

    def group(self, g):
        if self.number and self.p < 0:
            return 0
        if self.number and self.p == TILES - 1:
            return 5 * self.p + g
        return 5 * self.p + 1 + g

    def y_buf(self, g):
        return self.group(g) % 2 if self.number else (5 * self.par + 1 + g) % 2

    def last_group(self):
        if self.number and self.p == TILES:
            return 5 * (self.p - 1) + EXPERTS
        return 5 * self.p

    def last_buf(self):
        return self.last_group() % 2 if self.number else self.par


def periods(eng):
    for p in range(-3, 1):
        yield Period(p)
    with eng.Fori(1, TILES - 5, 2) as p:
        yield Period(p, 1)
        yield Period(p + 1, 0)
    for p in range(TILES - 4, TILES + 1):
        yield Period(p)


def build_program(nc, x, A, Bm, Cm, ln1_w, ln1_b, ln2_w, ln2_b, W1, b1, W2, b2,
                  gate_w, gate_b, ew1, eb1, ew2, eb2, out):
    ctx = ExitStack()

    def sb(name, shape, dt=F32):
        return ctx.enter_context(nc.sbuf_tensor(name, shape, dt))

    def sem(name):
        return ctx.enter_context(nc.semaphore(name))

    with ctx:
        up_ps = ctx.enter_context(nc.psum_tensor("up_ps", [P, 2, TOK], F32))
        y_ps = ctx.enter_context(nc.psum_tensor("y_ps", [P, TOK], F32))
        misc = ctx.enter_context(nc.psum_tensor("misc", [P, TOK], F32))
        misc_tok = misc[:, :].rearrange("p (b n) -> p b n", b=2)[:, :, 0:4 * C]

        w_raw = sb("w_raw", [C, COL_G + EXPERTS])
        w_sc = sb("w_sc", [C, COL_E])
        w_hi = sb("w_hi", [KR, WCOLS], F32R)
        w_lo = sb("w_lo", [C, WCOLS], F32R)
        b_row = sb("b_row", [1, WCOLS])
        b_hi = sb("b_hi", [1, WCOLS], F32R)
        b_lo = sb("b_lo", [1, WCOLS], F32R)
        b1_row = sb("b1_row", [1, HID])
        a_raw = sb("a_raw", [C, 2, C])
        a_hi = sb("a_hi", [C, 2, C], F32R)
        a_lo = sb("a_lo", [C, 2, C], F32R)
        d_raw = sb("d_raw", [P, SLOTS, C])
        d_hi = sb("d_hi", [P, SLOTS, C], F32R)
        d_lo = sb("d_lo", [P, SLOTS, C], F32R)
        b2_col = sb("b2_col", [C, 1 + EXPERTS])
        ln_col = sb("ln_col", [C, 4])
        ident = sb("ident", [P, P])
        neg_half = sb("neg_half", [P, SUBS])
        euler = sb("euler", [P, SUBS * EXPERTS])
        before = sb("before", [P, EXPERTS, EXPERTS])
        x_in = sb("x_in", [P, 2, SUBS, C])
        x_n = sb("x_n", [P, SUBS, C])
        xr = sb("xr", [P, SUBS, C])
        xr_n = sb("xr_n", [P, SUBS, C])
        x_xr = sb("x_xr", [P, SUBS, C])
        acc = sb("acc", [P, 2, SUBS, C])
        acc_n = sb("acc_n", [P, SUBS, C])
        weighted = sb("weighted", [P, SUBS, C])
        out_sb = sb("out_sb", [P, 2, SUBS, C])
        stats = sb("stats", [P, 3, SUBS, 6])
        apart = sb("apart", [P, 3, SUBS])
        mean2 = sb("mean2", [P, 3, SUBS])
        sq_dev = sb("sq_dev", [P, 3, SUBS])
        neg_mean = sb("neg_mean", [P, 3, SUBS])
        var_eps = sb("var_eps", [P, 3, SUBS])
        rstd = sb("rstd", [P, 3, SUBS])
        x_hi = sb("x_hi", [KR, TOK], F32R)
        x_lo = sb("x_lo", [C, TOK], F32R)
        h_hi = sb("h_hi", [C, TOK], F32R)
        h_lo = sb("h_lo", [C, TOK], F32R)
        y_hi = sb("y_hi", [KR, TOK], F32R)
        y_lo = sb("y_lo", [C, TOK], F32R)
        t_hi = sb("t_hi", [KR, 2, TOK], F32R)
        t_lo = sb("t_lo", [C, 2, TOK], F32R)
        g = sb("g", [P, 3, TOK])
        g_hi = sb("g_hi", [P, 3, TOK], F32R)
        g_lo = sb("g_lo", [P, 3, TOK], F32R)
        y_sb = sb("y_sb", [C, 2, TOK])
        score = sb("score", [P, SUBS, EXPERTS])
        top = sb("top", [P, SUBS])
        below = sb("below", [P, SUBS, EXPERTS])
        ex = sb("ex", [P, SUBS, EXPERTS])
        more = sb("more", [P, SUBS, EXPERTS, EXPERTS])
        same = sb("same", [P, SUBS, EXPERTS, EXPERTS])
        rank = sb("rank", [P, SUBS, EXPERTS])
        kept = sb("kept", [P, SUBS, EXPERTS])
        sum_all = sb("sum_all", [P, SUBS])
        sum_kept = sb("sum_kept", [P, SUBS])
        denom = sb("denom", [P, SUBS])
        inv = sb("inv", [P, SUBS])
        weight = sb("weight", [P, 2, SUBS, EXPERTS])

        w_loaded = sem("w_loaded")
        bias_rows = sem("bias_rows")
        x_loaded = [sem("x_loaded0"), sem("x_loaded1")]
        stored = [sem("stored0"), sem("stored1")]
        const_step = sem("const_step")
        prep = sem("prep")
        rows_set = sem("rows_set")
        bias_sums = sem("bias_sums")
        up_done, down_done = sem("up_done"), sem("down_done")
        x_turned, xr_turned, acc_turned = sem("x_turned"), sem("xr_turned"), sem("acc_turned")
        h_summed, xr_summed, scored = sem("h_summed"), sem("xr_summed"), sem("scored")
        y_turned = sem("y_turned")
        gelu_done, act_hi_done, y_copied = sem("gelu_done"), sem("act_hi_done"), sem("y_copied")
        x_hi_ok, h_hi_ok, y_hi_ok, t_hi_ok = sem("x_hi_ok"), sem("h_hi_ok"), sem("y_hi_ok"), sem("t_hi_ok")
        xr_copied = sem("xr_copied")
        dve_hi_done, lo_done = sem("dve_hi_done"), sem("lo_done")
        x_lo_ok, h_lo_ok, y_lo_ok, t_lo_ok = sem("x_lo_ok"), sem("h_lo_ok"), sem("y_lo_ok"), sem("t_lo_ok")
        stats_ok = [sem(f"stats_ok{k}") for k in range(3)]
        moments_ok = [sem(f"moments_ok{k}") for k in range(3)]
        x_xr_ok, x2_ok = sem("x_xr_ok"), sem("x2_ok")
        weighted_ok, summed = sem("weighted_ok"), sem("summed")
        gate_step = sem("gate_step")
        ln_step = [sem(f"ln_step{k}") for k in range(3)]
        normed = [sem(f"normed{k}") for k in range(3)]
        ex_ok = sem("ex_ok")

        W_PARTS = 18
        CONSTS = 8

        block = ctx.enter_context(nc.Block())

        @block.sync
        def _(sp):
            def load(t, par):
                sp.dma_start(x_in[:, par, :, :].rearrange("p s c -> p (s c)"), x[t, :, :]).then_inc(x_loaded[par], 16)

            def store(t, par):
                sp.wait_ge(summed, EXPERTS * t + EXPERTS)
                sp.dma_start(out[t, :, :], out_sb[:, par, :, :].rearrange("p s c -> p (s c)")).then_inc(stored[par], 16)

            def reload(t, par):
                sp.wait_ge(x_xr_ok, t - 1)
                load(t, par)

            load(0, 0)
            load(1, 1)
            for t in (2, 3, 4):
                reload(t, t % 2)
            with sp.Fori(1, TILES - 5, 2) as p:
                store(p - 1, 0)
                reload(p + 4, 1)
                store(p, 1)
                reload(p + 5, 0)
            for t in range(TILES - 5, TILES):
                store(t, t % 2)
            sp.wait_ge(stored[0], 16 * ((TILES + 1) // 2))
            sp.wait_ge(stored[1], 16 * (TILES // 2))

        @block.gpsimd
        def _(pool):
            pool.memset(ident[:, :], 0.0).then_inc(const_step, 1)
            pool.wait_ge(const_step, 1)
            pool.affine_select(out=ident[:, :], in_=ident[:, :], compare_op=ALU.not_equal, fill=1.0,
                               base=0, pattern=[[-1, P]], channel_multiplier=1).then_inc(const_step, 1)
            pool.memset(neg_half[:, :], -0.5).then_inc(const_step, 1)
            pool.memset(euler[:, :], 2.718281828459045).then_inc(const_step, 1)
            pool.memset(before[:, :, :], 0.0).then_inc(const_step, 1)
            pool.wait_ge(const_step, 5)
            for i in range(1, EXPERTS):
                pool.memset(before[:, i, 0:i], 1.0).then_inc(const_step, 1)
            pool.wait_ge(const_step, CONSTS)

            def per_token(ap):
                return ap.unsqueeze(2).to_broadcast([P, SUBS, C])

            def normalise(k, t, src, dst, turned, scale, eps):
                pool.wait_ge(moments_ok[k], t + 1)
                pool.tensor_tensor(neg_mean[:, k, :], mean2[:, k, :], neg_half[:, :], ALU.mult).then_inc(ln_step[k], 1)
                pool.tensor_scalar(var_eps[:, k, :], sq_dev[:, k, :], scale / C, eps, ALU.mult, ALU.add).then_inc(ln_step[k], 1)
                pool.wait_ge(ln_step[k], LN_STEPS * t + 2)
                pool.tensor_tensor(rstd[:, k, :], var_eps[:, k, :], neg_half[:, :], ALU.pow).then_inc(ln_step[k], 1)
                if not (isinstance(t, int) and t == 0):
                    pool.wait_ge(turned, t)
                pool.tensor_tensor(dst[:, :, :], src, per_token(neg_mean[:, k, :]), ALU.add).then_inc(ln_step[k], 1)
                pool.wait_ge(ln_step[k], LN_STEPS * t + 4)
                pool.tensor_tensor(dst[:, :, :], dst[:, :, :], per_token(rstd[:, k, :]), ALU.mult).then_inc(normed[k], 1)

            for q in periods(pool):
                if q.mlp:
                    normalise(2, q.p + 1, acc[:, 1 - q.par, :, :], acc_n, acc_turned, 1.0, EPS_T)
                if q.first_ln:
                    normalise(0, q.p + 3, x_in[:, 1 - q.par, :, :], x_n, x_turned, 1.0 + EPS_1, EPS_C * EPS_1)
                if q.recur:
                    normalise(1, q.p + 2, xr[:, :, :], xr_n, xr_turned, 1.0, EPS_1)
                if q.mlp:
                    t = q.p + 1
                    pool.wait_ge(gate_step, GATE_STEPS * t + 3)
                    pool.tensor_tensor(ex[:, :, :].rearrange("p s e -> p (s e)"), euler[:, :],
                                       below[:, :, :].rearrange("p s e -> p (s e)"), ALU.pow).then_inc(ex_ok, 1)

        @block.scalar
        def _(act):
            act.dma_start(w_raw[:, COL_B:COL_W1], Bm[:, :]).then_inc(w_loaded, 16)
            act.dma_start(w_raw[:, COL_W1:COL_E], W1[:, :]).then_inc(w_loaded, 16)
            act.dma_start(w_raw[:, COL_E:COL_G].rearrange("d (e h) -> d e h", e=EXPERTS),
                          ew1.rearrange("e d h -> d e h")).then_inc(w_loaded, 16)
            act.dma_start(w_raw[:, COL_G:COL_G + EXPERTS], gate_w[:, :]).then_inc(w_loaded, 16)
            act.dma_start(a_raw[:, 0, :], A[:, :]).then_inc(w_loaded, 16)
            act.dma_start(a_raw[:, 1, :], Cm[:, :]).then_inc(w_loaded, 16)
            act.dma_start(d_raw[:, 0:KB, :], W2.rearrange("(k p) c -> p k c", p=P)).then_inc(w_loaded, 16)
            for e in range(EXPERTS):
                act.dma_start(d_raw[:, KB * (1 + e):KB * (2 + e), :],
                              ew2[e, :, :].rearrange("(k p) c -> p k c", p=P)).then_inc(w_loaded, 16)
            act.dma_start(b2_col[:, 0:1], b2[:, :]).then_inc(w_loaded, 16)
            act.dma_start(b2_col[:, 1:1 + EXPERTS], eb2[:, :]).then_inc(w_loaded, 16)
            for i, v in enumerate((ln1_w, ln1_b, ln2_w, ln2_b)):
                act.dma_start(ln_col[:, i:i + 1], v[:, :]).then_inc(w_loaded, 16)
            act.dma_start(b1_row[:, :], b1[:, :]).then_inc(w_loaded, 16)
            act.dma_start(b_row[:, COL_E:COL_G], eb1[:, :]).then_inc(w_loaded, 16)
            act.dma_start(b_row[:, COL_G:COL_G + EXPERTS], gate_b[:, :]).then_inc(w_loaded, 16)
            act.wait_ge(prep, W_PARTS)
            act.dma_start(w_hi[C:C + 1, :].bitcast(F32), b_hi[:, :].bitcast(F32)).then_inc(bias_rows, 16)
            act.dma_start(w_hi[C + 1:KR, :].bitcast(F32), b_lo[:, :].bitcast(F32)).then_inc(bias_rows, 16)

            def gelu(q, s):
                n, r, u = q.unit(s), s % 3, q.up_buf(s)
                act.wait_ge(up_done, n + 1)
                if not (q.number and n < 3):
                    act.wait_ge(lo_done, n - 2)
                act.activation(g[:, r, :], up_ps[:, u, :], ACT.Gelu).then_inc(gelu_done, 1)

            def unit_hi(q, s):
                n, r = q.unit(s), s % 3
                act.wait_ge(gelu_done, n + 1)
                if not (q.number and n < 3):
                    act.wait_ge(down_done, n - 2)
                act.copy(g_hi[:, r, :], g[:, r, :]).then_inc(act_hi_done, 1)

            def hi_part(t, made, dst, done):
                act.wait_ge(made, t + 1)
                act.copy(dst, misc[0:C, :]).then_inc(done, 1)

            for q in periods(act):
                for s in range(SLOTS):
                    ahead = q.ahead(s)
                    if ahead:
                        gelu(*ahead)
                    if s == 6 and q.recur:
                        act.wait_ge(xr_summed, q.p + 3)
                        act.copy(xr[:, :, :].rearrange("p (b s) c -> p b (s c)", b=2), misc_tok).then_inc(xr_copied, 1)
                    if s == 7 and q.mlp:
                        hi_part(q.p + 1, acc_turned, t_hi[0:C, 1 - q.par, :], t_hi_ok)
                    if s == 11 and q.recur:
                        hi_part(q.p + 2, xr_turned, y_hi[0:C, :], y_hi_ok)
                    if s % KB == KB - 1 and q.has_unit(s):
                        grp = s // KB
                        n = q.group(grp)
                        act.wait_ge(down_done, q.unit(s) + 1)
                        if not (q.number and n < 2):
                            act.wait_ge(y_turned, n - 1)
                        for h in HALVES:
                            act.activation(y_sb[:, q.y_buf(grp), h], y_ps[0:C, h], ACT.Identity,
                                           bias=b2_col[:, grp:grp + 1]).then_inc(y_copied, 1)
                    if ahead and ahead[1] in HI_ON_ACT:
                        unit_hi(*ahead)
                    if s == 1 and q.recur:
                        hi_part(q.p + 2, x_turned, x_hi[0:C, :], x_hi_ok)
                    if s == 4 and q.recur:
                        hi_part(q.p + 2, h_summed, h_hi[:, :], h_hi_ok)

        @block.vector
        def _(dve):
            def f(ap):
                return ap.bitcast(F32)

            for rows in (x_hi[C:KR, :], y_hi[C:KR, :], t_hi[C:KR, 0, :], t_hi[C:KR, 1, :]):
                dve.memset(f(rows), 1.0).then_inc(rows_set, 1)
            for state in (h_hi, h_lo):
                dve.memset(f(state[:, :]), 0.0).then_inc(rows_set, 1)

            done = [0]

            def part(ins):
                done[0] += 1
                ins.then_inc(prep, 1)

            dve.wait_ge(w_loaded, 16 * 20)
            part(dve.tensor_scalar(w_sc[:, COL_B:COL_W1], w_raw[:, COL_B:COL_W1], ln_col[:, 0:1], None, ALU.mult))
            part(dve.tensor_scalar(w_sc[:, COL_W1:COL_E], w_raw[:, COL_W1:COL_E], ln_col[:, 2:3], None, ALU.mult))
            part(dve.memset(b_row[:, COL_G + EXPERTS:WCOLS], 0.0))
            part(dve.memset(f(w_lo[:, COL_G + EXPERTS:WCOLS]), 0.0))
            part(dve.tensor_copy(w_hi[0:C, COL_E:COL_G + EXPERTS], w_raw[:, COL_E:COL_G + EXPERTS]))
            part(dve.tensor_copy(w_lo[:, COL_G:COL_G + EXPERTS], w_raw[:, COL_G:COL_G + EXPERTS]))
            part(dve.tensor_copy(a_hi[:, :, :], a_raw[:, :, :]))
            part(dve.tensor_copy(d_hi[:, :, :], d_raw[:, :, :]))
            dve.wait_ge(prep, 2)
            part(dve.tensor_copy(w_hi[0:C, 0:COL_E], w_sc[:, :]))
            dve.wait_ge(prep, 9)
            part(dve.tensor_tensor(w_lo[:, 0:COL_E], w_sc[:, :], f(w_hi[0:C, 0:COL_E]), ALU.subtract))
            part(dve.tensor_tensor(w_lo[:, COL_E:COL_G], w_raw[:, COL_E:COL_G], f(w_hi[0:C, COL_E:COL_G]), ALU.subtract))
            part(dve.tensor_tensor(w_hi[0:C, COL_G + EXPERTS:WCOLS], w_raw[:, COL_G:COL_G + EXPERTS],
                                   f(w_hi[0:C, COL_G:COL_G + EXPERTS]), ALU.subtract))
            part(dve.tensor_tensor(a_lo[:, :, :], a_raw[:, :, :], f(a_hi[:, :, :]), ALU.subtract))
            part(dve.tensor_tensor(d_lo[:, :, :], d_raw[:, :, :], f(d_hi[:, :, :]), ALU.subtract))
            dve.wait_ge(bias_sums, 1)
            part(dve.tensor_copy(b_row[:, COL_B:COL_W1], misc[0:1, 0:C]))
            part(dve.tensor_tensor(b_row[:, COL_W1:COL_E], misc[0:1, BANK:BANK + HID], b1_row[:, :], ALU.add))
            dve.wait_ge(prep, 16)
            part(dve.tensor_copy(b_hi[:, :], b_row[:, :]))
            dve.wait_ge(prep, 17)
            part(dve.tensor_tensor(b_lo[:, :], b_row[:, :], f(b_hi[:, :]), ALU.subtract))
            assert done[0] == W_PARTS
            dve.wait_ge(const_step, CONSTS)

            def unit_lo(q, s):
                n, r = q.unit(s), s % 3
                if s in HI_ON_ACT:
                    dve.wait_ge(act_hi_done, q.before(s, HI_ON_ACT) + 1)
                    dve.tensor_tensor(g_lo[:, r, :], g[:, r, :], f(g_hi[:, r, :]), ALU.subtract).then_inc(lo_done, 1)
                else:
                    dve.wait_ge(gelu_done, n + 1)
                    if not (q.number and n < 3):
                        dve.wait_ge(down_done, n - 2)
                    dve.tensor_copy(g_hi[:, r, :], g[:, r, :]).then_inc(dve_hi_done, 1)
                    dve.wait_ge(dve_hi_done, q.before(s, HI_ON_DVE) + 1)
                    dve.tensor_tensor(g_lo[:, r, :], g[:, r, :], f(g_hi[:, r, :]), ALU.subtract).then_inc(lo_done, 1)

            def lo_part(t, hi_ok, hi, lo, lo_ok):
                dve.wait_ge(hi_ok, t + 1)
                dve.tensor_tensor(lo, misc[0:C, :], f(hi), ALU.subtract).then_inc(lo_ok, 1)

            def moments(k, t, src):
                for s in range(SUBS):
                    ins = dve.bn_stats(stats[:, k, s, :], src[:, s, :])
                ins.then_inc(stats_ok[k], 1)
                dve.wait_ge(stats_ok[k], MOMENT_STEPS * t + 1)
                mean_e, dev_e, mean_o, dev_o = (stats[:, k, :, i] for i in (1, 2, 4, 5))
                dve.tensor_tensor(apart[:, k, :], mean_e, mean_o, ALU.subtract).then_inc(stats_ok[k], 1)
                if not (isinstance(t, int) and t == 0):
                    dve.wait_ge(normed[k], t)
                dve.tensor_tensor(mean2[:, k, :], mean_e, mean_o, ALU.add)
                dve.wait_ge(stats_ok[k], MOMENT_STEPS * t + 2)
                dve.scalar_tensor_tensor(apart[:, k, :], in0=apart[:, k, :], scalar=C / 4, in1=apart[:, k, :],
                                         op0=ALU.mult, op1=ALU.mult)
                dve.tensor_tensor(sq_dev[:, k, :], dev_e, dev_o, ALU.add).then_inc(stats_ok[k], 1)
                dve.wait_ge(stats_ok[k], MOMENT_STEPS * t + 3)
                dve.tensor_tensor(sq_dev[:, k, :], sq_dev[:, k, :], apart[:, k, :], ALU.add).then_inc(moments_ok[k], 1)

            def tok4(ap):
                return ap.rearrange("p (b s) c -> p b s c", b=2)

            def combine(t, par, e, turned):
                w = weight[:, par, :, e].rearrange("p (b s) -> p b s", b=2).unsqueeze(3).to_broadcast([P, 2, 4, C])
                if not (isinstance(t, int) and t == 0 and e == 0):
                    dve.wait_ge(summed, EXPERTS * t + e)
                dve.wait_ge(y_turned, turned + 1)
                dve.tensor_tensor(tok4(weighted[:, :, :]), misc_tok.rearrange("p b (s c) -> p b s c", s=4), w,
                                  ALU.mult).then_inc(weighted_ok, 1)
                dve.wait_ge(weighted_ok, EXPERTS * t + e + 1)
                if e < EXPERTS - 1:
                    dst = acc
                else:
                    dst = out_sb
                    if not (isinstance(t, int) and t < 2):
                        dve.wait_ge(stored[par], 8 * (t - par))
                dve.tensor_tensor(dst[:, par, :, :], acc[:, par, :, :], weighted[:, :, :], ALU.add).then_inc(summed, 1)

            gate_at = [0]

            def step(ins, n):
                gate_at[0] = gate_at[0] % GATE_STEPS + 1
                assert gate_at[0] == n
                ins.then_inc(gate_step, 1)

            def per_sub(ap):
                return ap.unsqueeze(2).to_broadcast([P, SUBS, EXPERTS])

            def gate_ranks(t):
                after = lambda n: dve.wait_ge(gate_step, GATE_STEPS * t + n)
                pairs = [P, SUBS, EXPERTS, EXPERTS]
                this = score[:, :, :].unsqueeze(3).to_broadcast(pairs)
                other = score[:, :, :].unsqueeze(2).to_broadcast(pairs)
                dve.wait_ge(scored, t + 1)
                step(dve.tensor_reduce(score[:, :, :], misc[:, 0:SUBS * 2 * EXPERTS].rearrange(
                    "p (s l e) -> p s e l", s=SUBS, l=2), AX_X, ALU.add), 1)
                after(1)
                step(dve.tensor_reduce(top[:, :], score[:, :, :], AX_X, ALU.max), 2)
                after(2)
                step(dve.tensor_tensor(below[:, :, :], score[:, :, :], per_sub(top[:, :]), ALU.subtract), 3)
                step(dve.tensor_tensor(more[:, :, :, :], other, this, ALU.is_gt), 4)
                step(dve.tensor_tensor(same[:, :, :, :], other, this, ALU.is_equal), 5)
                after(5)
                first = before[:, :, :].unsqueeze(1).to_broadcast(pairs)
                step(dve.tensor_tensor(same[:, :, :, :], same[:, :, :, :], first, ALU.mult), 6)
                after(6)
                step(dve.tensor_tensor(more[:, :, :, :], more[:, :, :, :], same[:, :, :, :], ALU.add), 7)
                after(7)
                step(dve.tensor_reduce(rank[:, :, :], more[:, :, :, :], AX_X, ALU.add), 8)

            def gate_weights(t, par):
                after = lambda n: dve.wait_ge(gate_step, GATE_STEPS * t + n)
                after(8)
                dve.wait_ge(ex_ok, t + 1)
                step(dve.tensor_reduce(sum_all[:, :], ex[:, :, :], AX_X, ALU.add), 9)
                step(dve.scalar_tensor_tensor(kept[:, :, :], in0=rank[:, :, :], scalar=2.0, in1=ex[:, :, :],
                                              op0=ALU.is_lt, op1=ALU.mult), 10)
                after(10)
                step(dve.tensor_reduce(sum_kept[:, :], kept[:, :, :], AX_X, ALU.add), 11)
                after(11)
                step(dve.scalar_tensor_tensor(denom[:, :], in0=sum_all[:, :], scalar=1e-9, in1=sum_kept[:, :],
                                              op0=ALU.mult, op1=ALU.add), 12)
                after(12)
                step(dve.reciprocal(inv[:, :], denom[:, :]), 13)
                after(13)
                step(dve.tensor_tensor(weight[:, par, :, :], kept[:, :, :], per_sub(inv[:, :]), ALU.mult), 14)

            for q in periods(dve):
                te, tm, tp, tl = q.p, q.p + 1, q.p + 2, q.p + 3
                par, npar = q.par, 1 - q.par
                for s in range(SLOTS):
                    if s == 6 and q.recur:
                        dve.wait_ge(xr_copied, tp + 1)
                        dve.tensor_tensor(x_xr[:, :, :], xr[:, :, :], x_in[:, par, :, :], ALU.add).then_inc(x_xr_ok, 1)
                    if s == 7 and q.mlp:
                        lo_part(tm, t_hi_ok, t_hi[0:C, npar, :], t_lo[:, npar, :], t_lo_ok)
                    if s == 11 and q.recur:
                        lo_part(tp, y_hi_ok, y_hi[0:C, :], y_lo[:, :], y_lo_ok)
                    if q.ahead(s):
                        unit_lo(*q.ahead(s))
                    if s == 0 and q.final:
                        combine(te - 1, npar, EXPERTS - 1, q.last_group())
                    if s == 1 and q.recur:
                        lo_part(tp, x_hi_ok, x_hi[0:C, :], x_lo[:, :], x_lo_ok)
                    if s == 3 and q.mlp:
                        dve.wait_ge(y_turned, q.group(0) + 1)
                        dve.tensor_tensor(acc[:, npar, :, :].rearrange("p (b s) c -> p b (s c)", b=2), misc_tok,
                                          x_xr[:, :, :].rearrange("p (b s) c -> p b (s c)", b=2), ALU.add).then_inc(x2_ok, 1)
                        dve.wait_ge(x2_ok, tm + 1)
                        moments(2, tm, acc[:, npar, :, :])
                    if s == 4 and q.recur:
                        lo_part(tp, h_hi_ok, h_hi[:, :], h_lo[:, :], h_lo_ok)
                    if s == 5 and q.first_ln:
                        dve.wait_ge(x_loaded[npar], 8 * (tl - npar) + 16)
                        moments(0, tl, x_in[:, npar, :, :])
                    if s in TURN_EXPERT and q.experts:
                        e = TURN_EXPERT.index(s)
                        combine(te, par, e, q.group(e + 1))
                    if s == 6 and q.recur:
                        moments(1, tp, xr[:, :, :])
                    if s == 10 and q.mlp:
                        gate_ranks(tm)
                    if s == 2 and q.experts:
                        gate_weights(te, par)

        @block.tensor
        def _(pe):
            pe.wait_ge(w_loaded, 16 * 20)
            pe.matmul(misc[0:1, 0:C], ln_col[:, 1:2], w_raw[:, COL_B:COL_W1], start=True, stop=True)
            pe.matmul(misc[0:1, BANK:BANK + HID], ln_col[:, 3:4], w_raw[:, COL_W1:COL_E],
                      start=True, stop=True).then_inc(bias_sums, 1)
            pe.wait_ge(const_step, CONSTS)
            pe.wait_ge(prep, W_PARTS)
            pe.wait_ge(bias_rows, 32)
            pe.wait_ge(rows_set, 6)

            def product(dst, rows, terms):
                for i, (w, v) in enumerate(terms):
                    for h in HALVES:
                        ins = pe.matmul(dst[0:rows, h], w, v[:, h], start=(i == 0), stop=(i == len(terms) - 1))
                return ins

            def up(q, s):
                n = q.unit(s)
                if s < KB:
                    hi, lo, col = y_hi[:, :], y_lo[:, :], COL_W1 + P * s
                    if s == 0:
                        pe.wait_ge(y_lo_ok, q.p + 2)
                else:
                    hi, lo, col = t_hi[:, q.par, :], t_lo[:, q.par, :], COL_E + P * (s - KB)
                    if s == KB:
                        pe.wait_ge(t_lo_ok, q.p + 1)
                if not (q.number and n < 2):
                    pe.wait_ge(gelu_done, n - 1)
                c = slice(col, col + P)
                product(up_ps[:, q.up_buf(s), :], P, ((w_hi[:, c], hi), (w_hi[0:C, c], lo),
                                                      (w_lo[:, c], hi[0:C, :]))).then_inc(up_done, 1)

            def down(q, s):
                n, r, grp, k = q.unit(s), s % 3, s // KB, s % KB
                pe.wait_ge(lo_done, n + 1)
                terms = ((d_hi[:, s, :], g_hi[:, r, :]), (d_hi[:, s, :], g_lo[:, r, :]), (d_lo[:, s, :], g_hi[:, r, :]))
                for j, h in enumerate(HALVES):
                    if k == 0 and not (q.number and q.group(grp) == 0):
                        pe.wait_ge(y_copied, 2 * q.group(grp) - 1 + j)
                    for i, (w, v) in enumerate(terms):
                        ins = pe.matmul(y_ps[0:C, h], w, v[:, h], start=(k == 0 and i == 0), stop=(k == KB - 1 and i == 2))
                ins.then_inc(down_done, 1)

            freed = [None]

            def use_misc(q, release, value):
                if freed[0] is not None:
                    pe.wait_ge(*freed[0])
                freed[0] = (release, value)

            def to_channels(src):
                for s in range(SUBS):
                    ins = pe.transpose(misc[0:C, s * P:(s + 1) * P], src[:, s, :], ident[:, :])
                return ins

            def turn_y(n, buf):
                pe.wait_ge(y_copied, 2 * n + 2)
                for s in range(SUBS):
                    ins = pe.transpose(misc_tok[:, s // 4, (s % 4) * C:(s % 4 + 1) * C],
                                       y_sb[:, buf, s * P:(s + 1) * P], ident[0:C, 0:C])
                ins.then_inc(y_turned, 1)

            for q in periods(pe):
                te, tm, tp = q.p, q.p + 1, q.p + 2
                par, npar = q.par, 1 - q.par
                if not q.number:
                    freed[0] = (weighted_ok, EXPERTS * (te - 1) + 3)
                if q.number and te == TILES - 4:
                    freed[0] = (weighted_ok, EXPERTS * (te - 1) + 3)
                for s in range(SLOTS):
                    if q.ahead(s):
                        up(*q.ahead(s))
                    if s == 6 and q.recur:
                        use_misc(q, xr_copied, tp + 1)
                        pe.wait_ge(h_lo_ok, tp + 1)
                        for b in range(SUBS):
                            v = slice(b * P, (b + 1) * P)
                            dst = misc_tok[:, b // 4, (b % 4) * C:(b % 4 + 1) * C]
                            pe.matmul(dst, h_hi[:, v], a_hi[:, 1, :], start=True, stop=False)
                            pe.matmul(dst, h_lo[:, v], a_hi[:, 1, :], start=False, stop=False)
                            ins = pe.matmul(dst, h_hi[:, v], a_lo[:, 1, :], start=False, stop=True)
                        ins.then_inc(xr_summed, 1)
                    if s == 7 and q.mlp:
                        use_misc(q, t_lo_ok, tm + 1)
                        pe.wait_ge(normed[2], tm + 1)
                        to_channels(acc_n).then_inc(acc_turned, 1)
                    if s == 11 and q.recur:
                        use_misc(q, y_lo_ok, tp + 1)
                        pe.wait_ge(normed[1], tp + 1)
                        to_channels(xr_n).then_inc(xr_turned, 1)
                    if q.has_unit(s):
                        down(q, s)
                    if s == 0 and q.final:
                        use_misc(q, weighted_ok, EXPERTS * te)
                        turn_y(q.last_group(), q.last_buf())
                    if s == 1 and q.recur:
                        use_misc(q, x_lo_ok, tp + 1)
                        pe.wait_ge(normed[0], tp + 1)
                        to_channels(x_n).then_inc(x_turned, 1)
                    if s == 3 and q.mlp:
                        use_misc(q, x2_ok, tm + 1)
                        turn_y(q.group(0), q.y_buf(0))
                    if s == 4 and q.recur:
                        use_misc(q, h_lo_ok, tp + 1)
                        pe.wait_ge(x_lo_ok, tp + 1)
                        if not (q.number and tp == 0):
                            pe.wait_ge(h_lo_ok, tp)
                        c = slice(COL_B, COL_W1)
                        product(misc, C, ((w_hi[:, c], x_hi[:, :]), (w_hi[0:C, c], x_lo[:, :]), (w_lo[:, c], x_hi[0:C, :]),
                                          (a_hi[:, 0, :], h_hi[:, :]), (a_hi[:, 0, :], h_lo[:, :]),
                                          (a_lo[:, 0, :], h_hi[:, :]))).then_inc(h_summed, 1)
                    if s in TURN_EXPERT and q.experts:
                        e = TURN_EXPERT.index(s)
                        use_misc(q, weighted_ok, EXPERTS * te + e + 1)
                        turn_y(q.group(e + 1), q.y_buf(e + 1))
                    if s == 10 and q.mlp:
                        use_misc(q, gate_step, GATE_STEPS * tm + 1)
                        pe.wait_ge(t_lo_ok, tm + 1)
                        c = slice(COL_G, WCOLS)
                        for b in range(SUBS):
                            v = slice(b * P, (b + 1) * P)
                            dst = misc[:, 2 * EXPERTS * b:2 * EXPERTS * (b + 1)]
                            pe.matmul(dst, t_hi[:, npar, v], w_hi[:, c], start=True, stop=False)
                            ins = pe.matmul(dst, t_lo[:, npar, v], w_lo[:, c], start=False, stop=True)
                        ins.then_inc(scored, 1)


NAMES = ("x", "L0_conv_A", "L0_conv_Bm", "L0_conv_Cm", "L0_conv_ln1_w", "L0_conv_ln1_b", "L0_conv_ln2_w",
         "L0_conv_ln2_b", "L0_conv_W1", "L0_conv_b1", "L0_conv_W2", "L0_conv_b2", "L0_ffn_gate_w",
         "L0_ffn_gate_b", "L0_ffn_w1", "L0_ffn_b1", "L0_ffn_w2", "L0_ffn_b2")


def kernel(**inputs):
    import numpy as np
    import concourse.bacc as bacc
    from concourse.bass_utils import run_bass_kernel_spmd

    B, H, W, ch = inputs["x"].shape
    a = {n: np.asarray(inputs[n]) for n in NAMES}
    win = a["x"].reshape(B, H // WIN, WIN, W // WIN, WIN, ch).transpose(2, 4, 0, 1, 3, 5)
    a["x"] = win.reshape(TILES, P, SUBS * C)
    for n in ("L0_conv_ln1_w", "L0_conv_ln1_b", "L0_conv_ln2_w", "L0_conv_ln2_b", "L0_conv_b2"):
        a[n] = a[n].reshape(C, 1)
    for n in ("L0_conv_b1", "L0_ffn_gate_b", "L0_ffn_b1"):
        a[n] = a[n].reshape(1, -1)
    a["L0_ffn_b2"] = a["L0_ffn_b2"].T

    nc = bacc.Bacc("TRN2", target_bir_lowering=False, num_devices=1)
    arrays, args = {}, []
    for n in NAMES:
        v = np.ascontiguousarray(a[n])
        arrays[f"in_{n}"] = v
        args.append(nc.dram_tensor(f"in_{n}", v.shape, mybir.dt.from_np(v.dtype), kind="ExternalInput").ap())
    out = nc.dram_tensor("out_0", (TILES, P, SUBS * C), F32, kind="ExternalOutput").ap()
    build_program(nc, *args, out)
    r = run_bass_kernel_spmd(nc, [arrays], core_ids=[0])
    got = np.asarray(r.results[0]["out_0"]).reshape(WIN, WIN, B, H // WIN, W // WIN, ch)
    return np.ascontiguousarray(got.transpose(2, 3, 0, 4, 1, 5)).reshape(B, H, W, ch)
```

```python
from contextlib import ExitStack

import concourse.bass as bass
from concourse import mybir

F32 = mybir.dt.float32
F32R = mybir.dt.float32r
ALU = mybir.AluOpType
ACT = mybir.ActivationFunctionType
AX_X = mybir.AxisListType.X

P = 128
WIN = 7
TILES = WIN * WIN
SUBS = 8
C = 96
TOK = SUBS * P
BANK = 512
HID = 384
KB = HID // P
EXPERTS = 4
SLOTS = KB * (1 + EXPERTS)
KR = C + 2
AHEAD = 3
RING = 5
assert SLOTS % RING == 0 and SLOTS % 3 == 0
EARLY = 1

EPS_C, EPS_1, EPS_T = 1e-6, 1e-5, 1e-5

COL_B, COL_W1, COL_E = 0, C, C + HID
COL_G = COL_E + EXPERTS * HID
WCOLS = COL_G + 2 * EXPERTS

HI_ON_DVE = (2, 5, 8, 11, 14)
HI_ON_ACT = tuple(s for s in range(SLOTS) if s not in HI_ON_DVE)

TURN_EXPERT = (8, 10, 13)
HALVES = (slice(0, BANK), slice(BANK, TOK))

GATE_STEPS = 14
EXP_SUBS = 2
LOOP_FROM = 3
LN_STEPS = 4
FIRST_LN_AT = (6, 9, 10, 12)
NORM_STEPS = (len(FIRST_LN_AT), 1, 1)
MOMENT_STEPS = 4


class Period:

    def __init__(self, p, par=None):
        self.number = isinstance(p, int)
        self.p = p
        self.par = p % 2 if par is None else par
        has = lambda t: not self.number or 0 <= t < TILES
        self.final = has(p - 1)
        self.experts = has(p)
        self.mlp = has(p + 1)
        self.recur = has(p + 2)
        self.first_ln = has(p + 3)
        self.next_first_ln = has(p + 4) and not (self.number and p + 4 <= EARLY)
        self.runs_early = self.number and p + 3 == EARLY
        self.early_done = self.number and p + 2 == EARLY
        self.turn_xr_at = 4 if self.early_done else 9
        self.scores_at = SLOTS - 1 if self.early_done else 11

    def next(self):
        return Period(self.p + 1, 1 - self.par) if not self.number else Period(self.p + 1)

    def has_unit(self, s):
        return self.mlp if s < KB else self.experts

    def ahead(self, s):
        if s + AHEAD < SLOTS:
            return (self, s + AHEAD) if self.has_unit(s + AHEAD) else None
        return (self.next(), s + AHEAD - SLOTS) if self.recur else None

    def part_buf(self, s):
        return (self.unit(s) if self.number else KB + s) % RING

    def unit(self, s):
        if self.number and self.p < 0:
            return s
        if self.number and self.p == TILES - 1:
            return KB + SLOTS * self.p - KB + s
        return SLOTS * self.p + KB + s

    def up_buf(self, s):
        if self.number and self.p == TILES - 1:
            return self.unit(s) % 2
        return (KB + SLOTS * self.par + s) % 2

    def before(self, s, slots):
        mlp, here = sum(x < KB for x in slots), sum(x < s for x in slots)
        if self.number and self.p < 0:
            return here
        if self.number and self.p == TILES - 1:
            return len(slots) * self.p + here
        return len(slots) * self.p + mlp + here

    def group(self, g):
        if self.number and self.p < 0:
            return 0
        if self.number and self.p == TILES - 1:
            return 5 * self.p + g
        return 5 * self.p + 1 + g

    def y_buf(self, g):
        return self.group(g) % 2 if self.number else (5 * self.par + 1 + g) % 2

    def last_group(self):
        if self.number and self.p == TILES:
            return 5 * (self.p - 1) + EXPERTS
        return 5 * self.p

    def last_buf(self):
        return self.last_group() % 2 if self.number else self.par


def periods(eng):
    for p in range(-3, LOOP_FROM):
        yield Period(p)
    with eng.Fori(LOOP_FROM, TILES - 5, 2) as p:
        yield Period(p, 1)
        yield Period(p + 1, 0)
    for p in range(TILES - 4, TILES + 1):
        yield Period(p)


def build_program(nc, x, up_w, state_w, down_w, up_b, down_b, ln_wb, out):
    ctx = ExitStack()

    def sb(name, shape, dt=F32):
        return ctx.enter_context(nc.sbuf_tensor(name, shape, dt))

    def sem(name):
        return ctx.enter_context(nc.semaphore(name))

    with ctx:
        up_ps = ctx.enter_context(nc.psum_tensor("up_ps", [P, 2, TOK], F32))
        y_ps = ctx.enter_context(nc.psum_tensor("y_ps", [P, TOK], F32))
        misc = ctx.enter_context(nc.psum_tensor("misc", [P, TOK], F32))
        misc_xr = misc[:, :].rearrange("p (b n) -> p b n", b=2)[:, :, 0:4 * C].rearrange(
            "p b (s l c) -> p b s l c", s=2, l=2)
        misc_tok = misc[:, :].rearrange("p (b n) -> p b n", b=2)[:, :, 0:4 * C]

        w_raw = sb("w_raw", [C, COL_G + EXPERTS])
        w_sc = sb("w_sc", [C, COL_E])
        w_hi = sb("w_hi", [KR, WCOLS], F32R)
        w_lo = sb("w_lo", [C, WCOLS], F32R)
        a_raw = sb("a_raw", [C, 2, C])
        a_parts = sb("a_parts", [C, 2, 2, C], F32R)
        a_hi, a_lo = a_parts[:, 0, :, :], a_parts[:, 1, :, :]
        d_raw = sb("d_raw", [P, SLOTS, C])
        d_hi = sb("d_hi", [P, SLOTS, C], F32R)
        d_lo = sb("d_lo", [P, SLOTS, C], F32R)
        b2_col = sb("b2_col", [C, 1 + EXPERTS])
        ln_col = sb("ln_col", [C, 4])
        ident = sb("ident", [P, P])
        neg_half = sb("neg_half", [P, SUBS])
        euler = sb("euler", [P, EXP_SUBS * EXPERTS])
        before = sb("before", [P, EXPERTS, EXPERTS])
        x_in = sb("x_in", [P, 2, SUBS, C])
        x_n = sb("x_n", [P, SUBS, C])
        xr = sb("xr", [P, SUBS, C])
        xr_n = sb("xr_n", [P, SUBS, C])
        x_xr = sb("x_xr", [P, SUBS, C])
        acc = sb("acc", [P, 2, SUBS, C])
        acc_n = sb("acc_n", [P, SUBS, C])
        weighted = sb("weighted", [P, SUBS, C])
        out_sb = sb("out_sb", [P, 2, SUBS, C])
        stats = sb("stats", [P, 3, SUBS, 6])
        apart = sb("apart", [P, 3, SUBS])
        mean2 = sb("mean2", [P, 3, SUBS])
        sq_dev = sb("sq_dev", [P, 3, SUBS])
        neg_mean = sb("neg_mean", [P, 3, SUBS])
        var_eps = sb("var_eps", [P, 3, SUBS])
        rstd = sb("rstd", [P, 3, SUBS])
        shift = sb("shift", [P, SUBS])
        x_hi = sb("x_hi", [KR, TOK], F32R)
        x_lo = sb("x_lo", [C, TOK], F32R)
        h_hi = sb("h_hi", [C, TOK], F32R)
        h_lo = sb("h_lo", [C, TOK], F32R)
        y_hi = sb("y_hi", [KR, TOK], F32R)
        y_lo = sb("y_lo", [C, TOK], F32R)
        t_hi = sb("t_hi", [KR, 2, TOK], F32R)
        t_lo = sb("t_lo", [C, 2, TOK], F32R)
        g = sb("g", [P, 3, TOK])
        g_hi = sb("g_hi", [P, RING, TOK], F32R)
        g_lo = sb("g_lo", [P, RING, TOK], F32R)
        b_row, b_hi, b_lo = (ap[0:1, 0:2, :].rearrange("p r t -> p (r t)")[:, 0:WCOLS] for ap in (g, g_hi, g_lo))
        y_sb = sb("y_sb", [C, 2, TOK])
        score = sb("score", [P, SUBS, EXPERTS])
        top = sb("top", [P, SUBS])
        below = sb("below", [P, SUBS, EXPERTS])
        ex = sb("ex", [P, SUBS, EXPERTS])
        more = sb("more", [P, SUBS, EXPERTS, EXPERTS])
        same = sb("same", [P, SUBS, EXPERTS, EXPERTS])
        rank = sb("rank", [P, SUBS, EXPERTS])
        kept = sb("kept", [P, SUBS, EXPERTS])
        sum_all = sb("sum_all", [P, SUBS])
        sum_kept = sb("sum_kept", [P, SUBS])
        denom = sb("denom", [P, SUBS])
        inv = sb("inv", [P, SUBS])
        weight = sb("weight", [P, 2, SUBS, EXPERTS])

        first_loaded, later_loaded = sem("first_loaded"), sem("later_loaded")
        x_loaded = [sem("x_loaded0"), sem("x_loaded1")]
        stored = [sem("stored0"), sem("stored1")]
        const_step = sem("const_step")
        rows_set = sem("rows_set")
        prep, later_prep, act_prep = sem("prep"), sem("later_prep"), sem("act_prep")
        bias_sums = sem("bias_sums")
        first_rows, later_rows = sem("first_rows"), sem("later_rows")
        up_done, down_done = sem("up_done"), sem("down_done")
        x_turned, xr_turned, acc_turned = sem("x_turned"), sem("xr_turned"), sem("acc_turned")
        h_summed, xr_summed, scored = sem("h_summed"), sem("xr_summed"), sem("scored")
        y_turned = sem("y_turned")
        gelu_done, act_hi_done, y_copied = sem("gelu_done"), sem("act_hi_done"), sem("y_copied")
        x_hi_ok, h_hi_ok, y_hi_ok, t_hi_ok = sem("x_hi_ok"), sem("h_hi_ok"), sem("y_hi_ok"), sem("t_hi_ok")
        xr_copied = sem("xr_copied")
        dve_hi_done, lo_done = sem("dve_hi_done"), sem("lo_done")
        x_lo_ok, h_lo_ok, y_lo_ok, t_lo_ok = sem("x_lo_ok"), sem("h_lo_ok"), sem("y_lo_ok"), sem("t_lo_ok")
        stats_ok = [sem(f"stats_ok{k}") for k in range(3)]
        moments_ok = [sem(f"moments_ok{k}") for k in range(3)]
        x_xr_ok, x2_ok = sem("x_xr_ok"), sem("x2_ok")
        weighted_ok, summed = sem("weighted_ok"), sem("summed")
        gate_step = sem("gate_step")
        ln_step = [sem(f"ln_step{k}") for k in range(3)]
        normed = [sem(f"normed{k}") for k in range(3)]
        ex_ok = sem("ex_ok")

        FIRST_LOADS, LATER_LOADS = 5, 3
        PREP_STEPS = 10
        ACT_STEPS = 3
        LATER_STEPS = 3
        LATER_BIAS_STEPS = 5
        ONES_ROWS = 4
        CONSTS = 8

        block = ctx.enter_context(nc.Block())

        @block.sync
        def _(sp):
            def load(t, par):
                sp.dma_start(x_in[:, par, :, :].rearrange("p s c -> p (s c)"), x[t, :, :]).then_inc(x_loaded[par], 16)

            def store(t, par):
                sp.wait_ge(summed, EXPERTS * t + EXPERTS)
                sp.dma_start(out[t, :, :], out_sb[:, par, :, :].rearrange("p s c -> p (s c)")).then_inc(stored[par], 16)

            def reload(t, par):
                sp.wait_ge(x_xr_ok, t - 1)
                load(t, par)

            load(0, 0)
            load(1, 1)
            for t in (2, 3, 4):
                reload(t, t % 2)
            with sp.Fori(1, TILES - 5, 2) as p:
                store(p - 1, 0)
                reload(p + 4, 1)
                store(p, 1)
                reload(p + 5, 0)
            for t in range(TILES - 5, TILES):
                store(t, t % 2)
            sp.wait_ge(stored[0], 16 * ((TILES + 1) // 2))
            sp.wait_ge(stored[1], 16 * (TILES // 2))

        @block.gpsimd
        def _(pool):
            pool.memset(ident[:, :], 0.0).then_inc(const_step, 1)
            pool.memset(neg_half[:, :], -0.5).then_inc(const_step, 1)
            pool.wait_ge(const_step, 2)
            pool.affine_select(out=ident[:, :], in_=ident[:, :], compare_op=ALU.not_equal, fill=1.0,
                               base=0, pattern=[[-1, P]], channel_multiplier=1).then_inc(const_step, 1)
            pool.memset(euler[:, :], 2.718281828459045).then_inc(const_step, 1)
            pool.memset(before[:, :, :], 0.0).then_inc(const_step, 1)
            pool.wait_ge(const_step, 5)
            for i in range(1, EXPERTS):
                pool.memset(before[:, i, 0:i], 1.0).then_inc(const_step, 1)
            pool.wait_ge(const_step, CONSTS)

            def per_token(ap):
                return ap.unsqueeze(2).to_broadcast([P, SUBS, C])

            def rstd_of(k, t, scale, eps):
                pool.wait_ge(moments_ok[k], t + 1)
                if not (isinstance(t, int) and t == 0):
                    pool.wait_ge(normed[k], NORM_STEPS[k] * t)
                pool.tensor_tensor(neg_mean[:, k, :], mean2[:, k, :], neg_half[:, :], ALU.mult).then_inc(ln_step[k], 1)
                pool.tensor_scalar(var_eps[:, k, :], sq_dev[:, k, :], scale / C, eps, ALU.mult, ALU.add).then_inc(ln_step[k], 1)
                pool.wait_ge(ln_step[k], LN_STEPS * t + 2)
                pool.tensor_tensor(rstd[:, k, :], var_eps[:, k, :], neg_half[:, :], ALU.pow).then_inc(ln_step[k], 1)
                pool.wait_ge(ln_step[k], LN_STEPS * t + 3)

            def first_ln(t):
                rstd_of(0, t, 1.0 + EPS_1, EPS_C * EPS_1)
                pool.tensor_tensor(shift[:, :], neg_mean[:, 0, :], rstd[:, 0, :], ALU.mult).then_inc(ln_step[0], 1)

            def normalise(k, t, src, dst, turned):
                if not (isinstance(t, int) and t == 0):
                    pool.wait_ge(turned, t)
                pool.tensor_tensor(dst[:, :, :], src, per_token(neg_mean[:, k, :]), ALU.add).then_inc(ln_step[k], 1)
                pool.wait_ge(ln_step[k], LN_STEPS * t + 4)
                pool.tensor_tensor(dst[:, :, :], dst[:, :, :], per_token(rstd[:, k, :]), ALU.mult).then_inc(normed[k], 1)

            def second_ln(t):
                rstd_of(1, t, 1.0, EPS_1)
                normalise(1, t, xr[:, :, :], xr_n, xr_turned)

            for q in periods(pool):
                if q.runs_early:
                    first_ln(EARLY)
                    second_ln(0)
                if q.first_ln and not q.runs_early:
                    first_ln(q.p + 3)
                if q.early_done:
                    second_ln(EARLY)
                if q.mlp:
                    rstd_of(2, q.p + 1, 1.0, EPS_T)
                    normalise(2, q.p + 1, acc[:, 1 - q.par, :, :], acc_n, acc_turned)
                if q.recur and not (q.runs_early or q.early_done):
                    second_ln(q.p + 2)
                if q.mlp:
                    t = q.p + 1
                    pool.wait_ge(gate_step, GATE_STEPS * t + 3)
                    for b in range(0, SUBS, EXP_SUBS):
                        pool.tensor_tensor(ex[:, b:b + EXP_SUBS, :].rearrange("p s e -> p (s e)"), euler[:, :],
                                           below[:, b:b + EXP_SUBS, :].rearrange("p s e -> p (s e)"),
                                           ALU.pow).then_inc(ex_ok, 1)

        @block.scalar
        def _(act):
            act.dma_start(w_raw[:, COL_B:COL_W1], up_w[:, COL_B:COL_W1]).then_inc(first_loaded, 16)
            act.dma_start(ln_col[:, :], ln_wb[:, :]).then_inc(first_loaded, 16)
            act.dma_start(w_raw[:, COL_W1:COL_E], up_w[:, COL_W1:COL_E]).then_inc(first_loaded, 16)
            act.dma_start(a_raw[:, :, :], state_w[:, :, :]).then_inc(first_loaded, 16)
            act.dma_start(b_row[:, COL_W1:COL_G + EXPERTS], up_b[:, :]).then_inc(first_loaded, 16)
            act.dma_start(w_raw[:, COL_E:], up_w[:, COL_E:]).then_inc(later_loaded, 16)
            act.dma_start(d_raw[:, :, :], down_w.rearrange("(s p) c -> p s c", p=P)).then_inc(later_loaded, 16)
            act.dma_start(b2_col[:, :], down_b[:, :]).then_inc(later_loaded, 16)

            def first_ln(t, par, part):
                if part == 0:
                    act.wait_ge(ln_step[0], LN_STEPS * t + LN_STEPS)
                    if not (isinstance(t, int) and t == 0):
                        act.wait_ge(x_turned, t)
                n = SUBS // len(FIRST_LN_AT)
                for s in range(part * n, (part + 1) * n):
                    ins = act.activation(x_n[:, s, :], x_in[:, par, s, :], ACT.Identity,
                                         scale=rstd[:, 0, s:s + 1], bias=shift[:, s:s + 1])
                ins.then_inc(normed[0], 1)

            for part in range(len(FIRST_LN_AT)):
                first_ln(0, 0, part)

            def bias_rows(cols, done):
                act.dma_start(w_hi[C:C + 1, cols].bitcast(F32), b_hi[:, cols].bitcast(F32)).then_inc(done, 16)
                act.dma_start(w_hi[C + 1:KR, cols].bitcast(F32), b_lo[:, cols].bitcast(F32)).then_inc(done, 16)

            act.wait_ge(prep, PREP_STEPS)
            bias_rows(slice(0, COL_E), first_rows)
            act.wait_ge(later_loaded, 16 * LATER_LOADS)
            act.copy(w_hi[0:C, COL_E:COL_G + EXPERTS], w_raw[:, COL_E:]).then_inc(act_prep, 1)
            act.copy(w_lo[:, COL_G:COL_G + EXPERTS], w_raw[:, COL_G:]).then_inc(act_prep, 1)
            act.copy(d_hi[:, :, :], d_raw[:, :, :]).then_inc(act_prep, 1)

            def gelu(q, s):
                n, r, u = q.unit(s), s % 3, q.up_buf(s)
                if q.number and n == 0:
                    act.wait_ge(later_rows, 32)
                act.wait_ge(up_done, n + 1)
                if not (q.number and n < 3):
                    act.wait_ge(lo_done, n - 2)
                act.activation(g[:, r, :], up_ps[:, u, :], ACT.Gelu).then_inc(gelu_done, 1)

            def unit_hi(q, s):
                n, r, h = q.unit(s), s % 3, q.part_buf(s)
                act.wait_ge(gelu_done, n + 1)
                if not (q.number and n < RING):
                    act.wait_ge(down_done, n - RING + 1)
                act.copy(g_hi[:, h, :], g[:, r, :]).then_inc(act_hi_done, 1)

            def hi_part(t, made, dst, done):
                act.wait_ge(made, t + 1)
                act.copy(dst, misc[0:C, :]).then_inc(done, 1)

            for q in periods(act):
                for s in range(SLOTS):
                    ahead = q.ahead(s)
                    if ahead:
                        gelu(*ahead)
                    if s % KB == KB - 1 and q.has_unit(s):
                        grp = s // KB
                        n = q.group(grp)
                        act.wait_ge(down_done, q.unit(s) + 1)
                        if not (q.number and n < 2):
                            act.wait_ge(y_turned, n - 1)
                        for h in HALVES:
                            act.activation(y_sb[:, q.y_buf(grp), h], y_ps[0:C, h], ACT.Identity,
                                           bias=b2_col[:, grp:grp + 1]).then_inc(y_copied, 1)
                    if ahead and ahead[1] in HI_ON_ACT:
                        unit_hi(*ahead)
                    if s == q.turn_xr_at and q.recur:
                        hi_part(q.p + 2, xr_turned, y_hi[0:C, :], y_hi_ok)
                    if s == 7 and q.mlp:
                        hi_part(q.p + 1, acc_turned, t_hi[0:C, 1 - q.par, :], t_hi_ok)
                    if s in FIRST_LN_AT and q.first_ln and not (q.number and q.p + 3 <= EARLY):
                        first_ln(q.p + 3, 1 - q.par, FIRST_LN_AT.index(s))
                    if s == 1 and q.recur and not q.early_done:
                        hi_part(q.p + 2, x_turned, x_hi[0:C, :], x_hi_ok)
                        if q.runs_early:
                            for part in range(len(FIRST_LN_AT)):
                                first_ln(EARLY, EARLY % 2, part)
                    if s == 8 and q.runs_early:
                        hi_part(EARLY, x_turned, x_hi[0:C, :], x_hi_ok)
                        hi_part(EARLY, h_summed, h_hi[:, :], h_hi_ok)
                    if s == 4 and q.recur and not q.early_done:
                        hi_part(q.p + 2, h_summed, h_hi[:, :], h_hi_ok)
                        if q.number and q.p == -2:
                            act.wait_ge(later_prep, LATER_BIAS_STEPS)
                            bias_rows(slice(COL_E, WCOLS), later_rows)

        @block.vector
        def _(dve):
            def f(ap):
                return ap.bitcast(F32)

            def lo_part(t, hi_ok, hi, lo, lo_ok):
                dve.wait_ge(hi_ok, t + 1)
                dve.tensor_tensor(lo, misc[0:C, :], f(hi), ALU.subtract).then_inc(lo_ok, 1)

            def half_stats(k, src, half):
                for s in range(half * SUBS // 2, (half + 1) * SUBS // 2):
                    ins = dve.bn_stats(stats[:, k, s, :], src[:, s, :])
                ins.then_inc(stats_ok[k], 1)

            def moments(k, t):
                dve.wait_ge(stats_ok[k], MOMENT_STEPS * t + 2)
                mean_e, dev_e, mean_o, dev_o = (stats[:, k, :, i] for i in (1, 2, 4, 5))
                dve.tensor_tensor(apart[:, k, :], mean_e, mean_o, ALU.subtract).then_inc(stats_ok[k], 1)
                if not (isinstance(t, int) and t == 0):
                    dve.wait_ge(normed[k], NORM_STEPS[k] * t)
                dve.tensor_tensor(mean2[:, k, :], mean_e, mean_o, ALU.add)
                dve.wait_ge(stats_ok[k], MOMENT_STEPS * t + 3)
                dve.scalar_tensor_tensor(apart[:, k, :], in0=apart[:, k, :], scalar=C / 4, in1=apart[:, k, :],
                                         op0=ALU.mult, op1=ALU.mult)
                dve.tensor_tensor(sq_dev[:, k, :], dev_e, dev_o, ALU.add).then_inc(stats_ok[k], 1)
                dve.wait_ge(stats_ok[k], MOMENT_STEPS * t + 4)
                dve.tensor_tensor(sq_dev[:, k, :], sq_dev[:, k, :], apart[:, k, :], ALU.add).then_inc(moments_ok[k], 1)

            def all_moments(k, t, src):
                half_stats(k, src, 0)
                half_stats(k, src, 1)
                moments(k, t)

            def first_weights():
                dve.wait_ge(first_loaded, 16 * FIRST_LOADS)
                dve.tensor_scalar(w_sc[:, COL_B:COL_W1], w_raw[:, COL_B:COL_W1], ln_col[:, 0:1], None, ALU.mult).then_inc(prep, 1)
                dve.tensor_scalar(w_sc[:, COL_W1:], w_raw[:, COL_W1:COL_E], ln_col[:, 2:3], None, ALU.mult).then_inc(prep, 1)
                dve.wait_ge(bias_sums, 1)
                dve.tensor_copy(b_row[:, COL_B:COL_W1], misc[0:1, 0:C]).then_inc(prep, 1)
                dve.tensor_tensor(b_row[:, COL_W1:COL_E], misc[0:1, BANK:BANK + HID], b_row[:, COL_W1:COL_E],
                                  ALU.add).then_inc(prep, 1)
                dve.wait_ge(prep, 4)
                dve.tensor_copy(b_hi[:, 0:COL_E], b_row[:, 0:COL_E]).then_inc(prep, 1)
                dve.tensor_copy(w_hi[0:C, 0:COL_E], w_sc[:, :]).then_inc(prep, 1)
                dve.tensor_copy(a_hi[:, :, :], a_raw[:, :, :]).then_inc(prep, 1)
                dve.wait_ge(prep, 7)
                dve.tensor_tensor(b_lo[:, 0:COL_E], b_row[:, 0:COL_E], f(b_hi[:, 0:COL_E]), ALU.subtract).then_inc(prep, 1)
                dve.tensor_tensor(w_lo[:, 0:COL_E], w_sc[:, :], f(w_hi[0:C, 0:COL_E]), ALU.subtract).then_inc(prep, 1)
                dve.tensor_tensor(a_lo[:, :, :], a_raw[:, :, :], f(a_hi[:, :, :]), ALU.subtract).then_inc(prep, 1)

            def later_weights():
                dve.wait_ge(act_prep, ACT_STEPS)
                dve.tensor_tensor(w_lo[:, COL_E:COL_G], w_raw[:, COL_E:COL_G], f(w_hi[0:C, COL_E:COL_G]),
                                  ALU.subtract).then_inc(later_prep, 1)
                dve.tensor_tensor(w_hi[0:C, COL_G + EXPERTS:], w_raw[:, COL_G:],
                                  f(w_hi[0:C, COL_G:COL_G + EXPERTS]), ALU.subtract).then_inc(later_prep, 1)
                dve.tensor_tensor(d_lo[:, :, :], d_raw[:, :, :], f(d_hi[:, :, :]), ALU.subtract).then_inc(later_prep, 1)

            def later_bias():
                rest = slice(COL_E, WCOLS)
                dve.tensor_copy(b_hi[:, rest], b_row[:, rest]).then_inc(later_prep, 1)
                dve.wait_ge(later_prep, LATER_STEPS + 1)
                dve.tensor_tensor(b_lo[:, rest], b_row[:, rest], f(b_hi[:, rest]), ALU.subtract).then_inc(later_prep, 1)

            dve.memset(f(x_hi[C:KR, :]), 1.0).then_inc(rows_set, 1)
            dve.wait_ge(x_loaded[0], 16)
            all_moments(0, 0, x_in[:, 0, :, :])
            dve.memset(b_row[:, COL_G + EXPERTS:WCOLS], 0.0)
            dve.memset(f(w_lo[:, COL_G + EXPERTS:WCOLS]), 0.0)
            first_weights()
            dve.wait_ge(x_loaded[EARLY], 16)
            all_moments(0, EARLY, x_in[:, EARLY, :, :])
            for rows in (y_hi[C:KR, :], t_hi[C:KR, 0, :], t_hi[C:KR, 1, :]):
                dve.memset(f(rows), 1.0).then_inc(rows_set, 1)
            dve.wait_ge(const_step, CONSTS)

            def unit_lo(q, s):
                n, r, h = q.unit(s), s % 3, q.part_buf(s)
                if s in HI_ON_ACT:
                    dve.wait_ge(act_hi_done, q.before(s, HI_ON_ACT) + 1)
                else:
                    dve.wait_ge(gelu_done, n + 1)
                    if not (q.number and n < RING):
                        dve.wait_ge(down_done, n - RING + 1)
                    dve.tensor_copy(g_hi[:, h, :], g[:, r, :]).then_inc(dve_hi_done, 1)
                    dve.wait_ge(dve_hi_done, q.before(s, HI_ON_DVE) + 1)
                dve.tensor_tensor(g_lo[:, h, :], g[:, r, :], f(g_hi[:, h, :]), ALU.subtract).then_inc(lo_done, 1)

            def copy_xr(t, half):
                dve.wait_ge(xr_summed, 2 * t + 1 + half)
                if not (isinstance(t, int) and t == 0) and half == 0:
                    dve.wait_ge(normed[1], t)
                    dve.wait_ge(x_xr_ok, t)
                dve.tensor_reduce(xr[:, half * SUBS // 2:(half + 1) * SUBS // 2, :].rearrange("p (b s) c -> p b s c", b=2),
                                  misc_xr.rearrange("p b s l c -> p b s c l"), AX_X, ALU.add).then_inc(xr_copied, 1)
                dve.wait_ge(xr_copied, 2 * t + 1 + half)
                half_stats(1, xr, half)
                if half == 1:
                    moments(1, t)

            def tok4(ap):
                return ap.rearrange("p (b s) c -> p b s c", b=2)

            def combine(t, par, e, turned):
                w = weight[:, par, :, e].rearrange("p (b s) -> p b s", b=2).unsqueeze(3).to_broadcast([P, 2, 4, C])
                if not (isinstance(t, int) and t == 0 and e == 0):
                    dve.wait_ge(summed, EXPERTS * t + e)
                dve.wait_ge(y_turned, turned + 1)
                dve.tensor_tensor(tok4(weighted[:, :, :]), misc_tok.rearrange("p b (s c) -> p b s c", s=4), w,
                                  ALU.mult).then_inc(weighted_ok, 1)
                dve.wait_ge(weighted_ok, EXPERTS * t + e + 1)
                if e < EXPERTS - 1:
                    dst = acc
                else:
                    dst = out_sb
                    if not (isinstance(t, int) and t < 2):
                        dve.wait_ge(stored[par], 8 * (t - par))
                dve.tensor_tensor(dst[:, par, :, :], acc[:, par, :, :], weighted[:, :, :], ALU.add).then_inc(summed, 1)

            gate_at = [0]

            def step(ins, n):
                gate_at[0] = gate_at[0] % GATE_STEPS + 1
                assert gate_at[0] == n
                ins.then_inc(gate_step, 1)

            def per_sub(ap):
                return ap.unsqueeze(2).to_broadcast([P, SUBS, EXPERTS])

            def gate_ranks(t):
                after = lambda n: dve.wait_ge(gate_step, GATE_STEPS * t + n)
                pairs = [P, SUBS, EXPERTS, EXPERTS]
                this = score[:, :, :].unsqueeze(3).to_broadcast(pairs)
                other = score[:, :, :].unsqueeze(2).to_broadcast(pairs)
                dve.wait_ge(scored, t + 1)
                step(dve.tensor_reduce(score[:, :, :], misc[:, 0:SUBS * 2 * EXPERTS].rearrange(
                    "p (s l e) -> p s e l", s=SUBS, l=2), AX_X, ALU.add), 1)
                after(1)
                step(dve.tensor_reduce(top[:, :], score[:, :, :], AX_X, ALU.max), 2)
                after(2)
                step(dve.tensor_tensor(below[:, :, :], score[:, :, :], per_sub(top[:, :]), ALU.subtract), 3)
                step(dve.tensor_tensor(more[:, :, :, :], other, this, ALU.is_gt), 4)
                step(dve.tensor_tensor(same[:, :, :, :], other, this, ALU.is_equal), 5)
                after(5)
                first = before[:, :, :].unsqueeze(1).to_broadcast(pairs)
                step(dve.tensor_tensor(same[:, :, :, :], same[:, :, :, :], first, ALU.mult), 6)
                after(6)
                step(dve.tensor_tensor(more[:, :, :, :], more[:, :, :, :], same[:, :, :, :], ALU.add), 7)
                after(7)
                step(dve.tensor_reduce(rank[:, :, :], more[:, :, :, :], AX_X, ALU.add), 8)

            def gate_weights(t, par):
                after = lambda n: dve.wait_ge(gate_step, GATE_STEPS * t + n)
                after(8)
                dve.wait_ge(ex_ok, SUBS // EXP_SUBS * (t + 1))
                step(dve.tensor_reduce(sum_all[:, :], ex[:, :, :], AX_X, ALU.add), 9)
                step(dve.scalar_tensor_tensor(kept[:, :, :], in0=rank[:, :, :], scalar=2.0, in1=ex[:, :, :],
                                              op0=ALU.is_lt, op1=ALU.mult), 10)
                after(10)
                step(dve.tensor_reduce(sum_kept[:, :], kept[:, :, :], AX_X, ALU.add), 11)
                after(11)
                step(dve.scalar_tensor_tensor(denom[:, :], in0=sum_all[:, :], scalar=1e-9, in1=sum_kept[:, :],
                                              op0=ALU.mult, op1=ALU.add), 12)
                after(12)
                step(dve.reciprocal(inv[:, :], denom[:, :]), 13)
                after(13)
                step(dve.tensor_tensor(weight[:, par, :, :], kept[:, :, :], per_sub(inv[:, :]), ALU.mult), 14)

            for q in periods(dve):
                te, tm, tp, tl = q.p, q.p + 1, q.p + 2, q.p + 3
                par, npar = q.par, 1 - q.par
                for s in range(SLOTS):
                    if s == 0 and q.final:
                        combine(te - 1, npar, EXPERTS - 1, q.last_group())
                    if s == 3 and q.mlp:
                        dve.wait_ge(y_turned, q.group(0) + 1)
                        dve.tensor_tensor(acc[:, npar, :, :].rearrange("p (b s) c -> p b (s c)", b=2), misc_tok,
                                          x_xr[:, :, :].rearrange("p (b s) c -> p b (s c)", b=2), ALU.add).then_inc(x2_ok, 1)
                        dve.wait_ge(x2_ok, tm + 1)
                        all_moments(2, tm, acc[:, npar, :, :])
                    if s in (SLOTS - 2, SLOTS - 1) and q.runs_early:
                        copy_xr(EARLY, s - (SLOTS - 2))
                    if s in (5, 6) and q.recur and not q.early_done:
                        copy_xr(tp, s - 5)
                    if s in TURN_EXPERT and q.experts:
                        e = TURN_EXPERT.index(s)
                        combine(te, par, e, q.group(e + 1))
                    if s == q.scores_at and q.mlp:
                        gate_ranks(tm)
                    if s == q.turn_xr_at and q.recur:
                        lo_part(tp, y_hi_ok, y_hi[0:C, :], y_lo[:, :], y_lo_ok)
                    if s == 1 and q.recur and not q.early_done:
                        lo_part(tp, x_hi_ok, x_hi[0:C, :], x_lo[:, :], x_lo_ok)
                        if q.number and tp == 0:
                            later_weights()
                    if s == 8 and q.runs_early:
                        lo_part(EARLY, x_hi_ok, x_hi[0:C, :], x_lo[:, :], x_lo_ok)
                        lo_part(EARLY, h_hi_ok, h_hi[:, :], h_lo[:, :], h_lo_ok)
                    if s == 4 and q.recur and not q.early_done:
                        lo_part(tp, h_hi_ok, h_hi[:, :], h_lo[:, :], h_lo_ok)
                        if q.number and tp == 0:
                            later_bias()
                    if s == 7 and q.mlp:
                        lo_part(tm, t_hi_ok, t_hi[0:C, npar, :], t_lo[:, npar, :], t_lo_ok)
                    if q.ahead(s):
                        unit_lo(*q.ahead(s))
                    if s == 12 and q.next_first_ln:
                        dve.wait_ge(x_loaded[par], 8 * (tl + 1 - par) + 16)
                        all_moments(0, tl + 1, x_in[:, par, :, :])
                    if s == 7 and q.recur:
                        dve.wait_ge(xr_copied, 2 * tp + 2)
                        dve.tensor_tensor(x_xr[:, :, :], xr[:, :, :], x_in[:, par, :, :], ALU.add).then_inc(x_xr_ok, 1)
                    if s == 2 and q.experts:
                        gate_weights(te, par)

        @block.tensor
        def _(pe):
            pe.wait_ge(first_loaded, 16 * FIRST_LOADS)
            pe.matmul(misc[0:1, 0:C], ln_col[:, 1:2], w_raw[:, COL_B:COL_W1], start=True, stop=True)
            pe.matmul(misc[0:1, BANK:BANK + HID], ln_col[:, 3:4], w_raw[:, COL_W1:COL_E],
                      start=True, stop=True).then_inc(bias_sums, 1)
            pe.wait_ge(const_step, CONSTS)

            def product(dst, rows, terms):
                for i, (w, v) in enumerate(terms):
                    for h in HALVES:
                        ins = pe.matmul(dst[0:rows, h], w, v[:, h], start=(i == 0), stop=(i == len(terms) - 1))
                return ins

            def up(q, s):
                n = q.unit(s)
                if q.number and n == 0:
                    pe.wait_ge(rows_set, ONES_ROWS)
                if s < KB:
                    hi, lo, col = y_hi[:, :], y_lo[:, :], COL_W1 + P * s
                    if s == 0:
                        pe.wait_ge(y_lo_ok, q.p + 2)
                else:
                    hi, lo, col = t_hi[:, q.par, :], t_lo[:, q.par, :], COL_E + P * (s - KB)
                    if s == KB:
                        pe.wait_ge(t_lo_ok, q.p + 1)
                if not (q.number and n < 2):
                    pe.wait_ge(gelu_done, n - 1)
                c = slice(col, col + P)
                product(up_ps[:, q.up_buf(s), :], P, ((w_hi[:, c], hi), (w_hi[0:C, c], lo),
                                                      (w_lo[:, c], hi[0:C, :]))).then_inc(up_done, 1)

            def down(q, s):
                n, r, grp, k = q.unit(s), q.part_buf(s), s // KB, s % KB
                if q.number and n == 0:
                    pe.wait_ge(later_prep, LATER_STEPS)
                pe.wait_ge(lo_done, n + 1)
                terms = ((d_hi[:, s, :], g_hi[:, r, :]), (d_hi[:, s, :], g_lo[:, r, :]), (d_lo[:, s, :], g_hi[:, r, :]))
                for j, h in enumerate(HALVES):
                    if k == 0 and not (q.number and q.group(grp) == 0):
                        pe.wait_ge(y_copied, 2 * q.group(grp) - 1 + j)
                    for i, (w, v) in enumerate(terms):
                        ins = pe.matmul(y_ps[0:C, h], w, v[:, h], start=(k == 0 and i == 0), stop=(k == KB - 1 and i == 2))
                ins.then_inc(down_done, 1)

            freed = [None]

            def use_misc(release, value):
                if freed[0] is not None:
                    pe.wait_ge(*freed[0])
                freed[0] = (release, value)

            def to_channels(src):
                for s in range(SUBS):
                    ins = pe.transpose(misc[0:C, s * P:(s + 1) * P], src[:, s, :], ident[:, :])
                return ins

            def turn_y(n, buf):
                pe.wait_ge(y_copied, 2 * n + 2)
                for s in range(SUBS):
                    ins = pe.transpose(misc_tok[:, s // 4, (s % 4) * C:(s % 4 + 1) * C],
                                       y_sb[:, buf, s * P:(s + 1) * P], ident[0:C, 0:C])
                ins.then_inc(y_turned, 1)

            def turn_x(t):
                use_misc(x_lo_ok, t + 1)
                if isinstance(t, int) and t == 0:
                    pe.wait_ge(prep, 4)
                pe.wait_ge(normed[0], NORM_STEPS[0] * (t + 1))
                to_channels(x_n).then_inc(x_turned, 1)

            def sum_h(t):
                use_misc(h_lo_ok, t + 1)
                pe.wait_ge(x_lo_ok, t + 1)
                c = slice(COL_B, COL_W1)
                terms = [(w_hi[:, c], x_hi[:, :]), (w_hi[0:C, c], x_lo[:, :]), (w_lo[:, c], x_hi[0:C, :])]
                if isinstance(t, int) and t == 0:
                    pe.wait_ge(prep, PREP_STEPS)
                    pe.wait_ge(first_rows, 32)
                else:
                    pe.wait_ge(h_lo_ok, t)
                    terms += [(a_hi[:, 0, :], h_hi[:, :]), (a_hi[:, 0, :], h_lo[:, :]), (a_lo[:, 0, :], h_hi[:, :])]
                product(misc, C, terms).then_inc(h_summed, 1)

            def sum_xr(t, half):
                use_misc(xr_copied, 2 * t + 1 + half)
                if half == 0:
                    pe.wait_ge(h_lo_ok, t + 1)
                for i in range(SUBS // 2):
                    b = half * SUBS // 2 + i
                    v = slice(b * P, (b + 1) * P)
                    pe.matmul(misc_xr[:, i // 2, i % 2, :, :], h_hi[:, v], a_parts[:, :, 1, :], start=True, stop=False)
                    ins = pe.matmul(misc_xr[:, i // 2, i % 2, 0, :], h_lo[:, v], a_hi[:, 1, :], start=False, stop=True)
                ins.then_inc(xr_summed, 1)

            for q in periods(pe):
                te, tm, tp = q.p, q.p + 1, q.p + 2
                par, npar = q.par, 1 - q.par
                if not q.number:
                    freed[0] = (weighted_ok, EXPERTS * (te - 1) + 3)
                if q.number and te == TILES - 4:
                    freed[0] = (weighted_ok, EXPERTS * (te - 1) + 3)
                for s in range(SLOTS):
                    if q.ahead(s):
                        up(*q.ahead(s))
                    if q.has_unit(s):
                        down(q, s)
                    if s == 0 and q.final:
                        use_misc(weighted_ok, EXPERTS * te)
                        turn_y(q.last_group(), q.last_buf())
                    if s == 1 and q.recur and not q.early_done:
                        turn_x(tp)
                    if s == 3 and q.mlp:
                        use_misc(x2_ok, tm + 1)
                        turn_y(q.group(0), q.y_buf(0))
                    if s == 4 and q.recur and not q.early_done:
                        sum_h(tp)
                    if s == 8 and q.runs_early:
                        turn_x(EARLY)
                        sum_h(EARLY)
                    if s in (SLOTS - 2, SLOTS - 1) and q.runs_early:
                        sum_xr(EARLY, s - (SLOTS - 2))
                    if s in (5, 6) and q.recur and not q.early_done:
                        sum_xr(tp, s - 5)
                    if s == 7 and q.mlp:
                        use_misc(t_lo_ok, tm + 1)
                        pe.wait_ge(normed[2], NORM_STEPS[2] * (tm + 1))
                        to_channels(acc_n).then_inc(acc_turned, 1)
                    if s == q.turn_xr_at and q.recur:
                        use_misc(y_lo_ok, tp + 1)
                        pe.wait_ge(normed[1], NORM_STEPS[1] * (tp + 1))
                        to_channels(xr_n).then_inc(xr_turned, 1)
                    if s in TURN_EXPERT and q.experts:
                        e = TURN_EXPERT.index(s)
                        use_misc(weighted_ok, EXPERTS * te + e + 1)
                        turn_y(q.group(e + 1), q.y_buf(e + 1))
                    if s == q.scores_at and q.mlp:
                        use_misc(gate_step, GATE_STEPS * tm + 1)
                        pe.wait_ge(t_lo_ok, tm + 1)
                        if q.number and tm == 0:
                            pe.wait_ge(later_rows, 32)
                        c = slice(COL_G, WCOLS)
                        for b in range(SUBS):
                            v = slice(b * P, (b + 1) * P)
                            dst = misc[:, 2 * EXPERTS * b:2 * EXPERTS * (b + 1)]
                            pe.matmul(dst, t_hi[:, npar, v], w_hi[:, c], start=True, stop=False)
                            ins = pe.matmul(dst, t_lo[:, npar, v], w_lo[:, c], start=False, stop=True)
                        ins.then_inc(scored, 1)


def kernel(**inputs):
    import numpy as np
    import concourse.bacc as bacc
    from concourse.bass_utils import run_bass_kernel_spmd

    a = {n: np.asarray(v) for n, v in inputs.items()}
    conv = lambda n: a["L0_conv_" + n]
    ffn = lambda n: a["L0_ffn_" + n]
    B, H, W, ch = a["x"].shape
    win = a["x"].reshape(B, H // WIN, WIN, W // WIN, WIN, ch).transpose(2, 4, 0, 1, 3, 5)
    laid = {
        "x": win.reshape(TILES, P, SUBS * C),
        "up_w": np.concatenate([conv("Bm"), conv("W1"), *ffn("w1"), ffn("gate_w")], axis=1),
        "state_w": np.stack([conv("A"), conv("Cm")], axis=1),
        "down_w": np.concatenate([conv("W2"), *ffn("w2")], axis=0),
        "up_b": np.concatenate([conv("b1"), *ffn("b1"), ffn("gate_b")]).reshape(1, -1),
        "down_b": np.stack([conv("b2"), *ffn("b2")], axis=1),
        "ln_wb": np.stack([conv(n) for n in ("ln1_w", "ln1_b", "ln2_w", "ln2_b")], axis=1),
    }

    nc = bacc.Bacc("TRN2", target_bir_lowering=False, num_devices=1)
    arrays, args = {}, []
    for n, v in laid.items():
        v = np.ascontiguousarray(v)
        arrays[f"in_{n}"] = v
        args.append(nc.dram_tensor(f"in_{n}", v.shape, mybir.dt.from_np(v.dtype), kind="ExternalInput").ap())
    out = nc.dram_tensor("out_0", (TILES, P, SUBS * C), F32, kind="ExternalOutput").ap()
    build_program(nc, *args, out)
    r = run_bass_kernel_spmd(nc, [arrays], core_ids=[0])
    got = np.asarray(r.results[0]["out_0"]).reshape(WIN, WIN, B, H // WIN, W // WIN, ch)
    return np.ascontiguousarray(got.transpose(2, 3, 0, 4, 1, 5)).reshape(B, H, W, ch)
```
